# Optimizing a Trainium2 kernel written in Bass

```python
import numpy as np
import jax
import jax.numpy as jnp

def _softmax(x, axis=-1):
    return jax.nn.softmax(x, axis=axis)

def _gelu(x):
    return jax.nn.gelu(x, approximate=True)

def _silu(x):
    return jax.nn.silu(x)

def _sigmoid(x):
    return jax.nn.sigmoid(x)

def _layernorm(x, axis=-1, eps=1e-05):
    m = jnp.mean(x, axis=axis, keepdims=True)
    v = jnp.var(x, axis=axis, keepdims=True)
    return (x - m) / jnp.sqrt(v + eps)

def _scatter_add(tgt, idx, src, axis=0):
    return tgt.at[idx].add(src)

def _segment_sum(src, seg, n):
    return jax.ops.segment_sum(src, seg, n)
kernel_name = 'mk_gnn_resnorm_d4_gnn_r64_725a05'

def setup_inputs(seed: int=0):
    np.random.seed(seed)
    _w = jnp.asarray

    def _rec_inputs():
        import jax
        import jax.numpy as jnp
        _gk = jax.random.key(seed)
        x = -0.0003713 + 1 * jax.random.normal(jax.random.fold_in(_gk, 1), (50000, 128), jnp.float32)
        src = jax.random.randint(jax.random.fold_in(_gk, 2), (25000,), 0, 50000, jnp.int32)
        dst = jnp.minimum((50000 * jax.random.uniform(jax.random.fold_in(_gk, 3), (25000,)) ** 2.0).astype(jnp.int32), 49999)
        _o = jnp.argsort(dst, stable=True)
        src = src[_o]
        dst = dst[_o]
        return (x, src, dst)
    x, src, dst = _rec_inputs()

    def _L0_gnn_setup():
        import jax, jax.numpy as jnp
        import numpy as np
        N_NODES = 100000
        N_EDGES = 25000
        IN_F, HID_F, OUT_F = (128, 256, 128)
        key = jax.random.key(seed)
        ks = jax.random.split(key, 12)
        inp = {'x': jax.random.normal(ks[0], (N_NODES, IN_F), dtype=jnp.float32), 'src': jax.random.randint(ks[1], (N_EDGES,), 0, N_NODES, dtype=jnp.int32), 'dst': jax.random.randint(ks[2], (N_EDGES,), 0, N_NODES, dtype=jnp.int32), 'Ws0': jax.random.normal(ks[3], (IN_F, HID_F), dtype=jnp.float32) / np.sqrt(IN_F), 'Wn0': jax.random.normal(ks[4], (IN_F, HID_F), dtype=jnp.float32) / np.sqrt(IN_F), 'b0': jax.random.normal(ks[5], (HID_F,), dtype=jnp.float32) * 0.01, 'Ws1': jax.random.normal(ks[6], (HID_F, HID_F), dtype=jnp.float32) / np.sqrt(HID_F), 'Wn1': jax.random.normal(ks[7], (HID_F, HID_F), dtype=jnp.float32) / np.sqrt(HID_F), 'b1': jax.random.normal(ks[8], (HID_F,), dtype=jnp.float32) * 0.01, 'Ws2': jax.random.normal(ks[9], (HID_F, OUT_F), dtype=jnp.float32) / np.sqrt(HID_F), 'Wn2': jax.random.normal(ks[10], (HID_F, OUT_F), dtype=jnp.float32) / np.sqrt(HID_F), 'b2': jax.random.normal(ks[11], (OUT_F,), dtype=jnp.float32) * 0.01}
        return inp
    _L0_gnn_all = _L0_gnn_setup()
    _L0_gnn_in = {k: v for k, v in _L0_gnn_all.items() if k in ('Ws0', 'Wn0', 'b0', 'Ws1', 'Wn1', 'b1', 'Ws2', 'Wn2', 'b2')}
    del _L0_gnn_all

    def _L1_gnn_setup():
        import jax, jax.numpy as jnp
        import numpy as np
        N, E = (50000, 12500)
        IN_DIM, HC, OUT_DIM = (128, 64, 128)
        NEG_SLOPE = 0.2
        EPS = 1e-05

        def gat_conv(x, src, dst, W, att_src, att_dst, bias, heads, C, concat):
            n = x.shape[0]
            h = (x @ W).reshape(n, heads, C)
            a_src = jnp.einsum('nhc,hc->nh', h, att_src)
            a_dst = jnp.einsum('nhc,hc->nh', h, att_dst)
            e = jax.nn.leaky_relu(a_src[src] + a_dst[dst], NEG_SLOPE)
            emax = jax.ops.segment_max(e, dst, num_segments=n)
            ex = jnp.exp(e - emax[dst])
            denom = jax.ops.segment_sum(ex, dst, num_segments=n)
            alpha = ex / (denom[dst] + 1e-16)
            out = jax.ops.segment_sum(h[src] * alpha[:, :, None], dst, num_segments=n)
            out = out.reshape(n, heads * C) if concat else out.mean(axis=1)
            return out + bias

        def graph_layernorm(x, w, b):
            mean = x.mean()
            xc = x - mean
            var = (xc * xc).mean()
            return xc * jax.lax.rsqrt(var + EPS) * w + b
        key = jax.random.key(seed)
        ks = jax.random.split(key, 10)
        s = 0.1
        return {'x': jax.random.normal(ks[0], (N, IN_DIM), jnp.float32), 'edge_index': jax.random.randint(ks[1], (2, E), 0, N, dtype=jnp.int32), 'W1': jax.random.normal(ks[2], (IN_DIM, 2 * HC), jnp.float32) * s, 'att_src1': jax.random.normal(ks[3], (2, HC), jnp.float32) * s, 'att_dst1': jax.random.normal(ks[4], (2, HC), jnp.float32) * s, 'b1': jnp.zeros((2 * HC,), jnp.float32), 'ln1_w': jnp.ones((2 * HC,), jnp.float32), 'ln1_b': jnp.zeros((2 * HC,), jnp.float32), 'W2': jax.random.normal(ks[5], (2 * HC, OUT_DIM), jnp.float32) * s, 'att_src2': jax.random.normal(ks[6], (1, OUT_DIM), jnp.float32) * s, 'att_dst2': jax.random.normal(ks[7], (1, OUT_DIM), jnp.float32) * s, 'b2': jnp.zeros((OUT_DIM,), jnp.float32), 'ln2_w': jnp.ones((OUT_DIM,), jnp.float32), 'ln2_b': jnp.zeros((OUT_DIM,), jnp.float32)}
    _L1_gnn_all = _L1_gnn_setup()
    _L1_gnn_in = {k: v for k, v in _L1_gnn_all.items() if k in ('W1', 'att_src1', 'att_dst1', 'b1', 'ln1_w', 'ln1_b', 'W2', 'att_src2', 'att_dst2', 'b2', 'ln2_w', 'ln2_b')}
    del _L1_gnn_all

    def _L2_gnn_setup():
        import jax, jax.numpy as jnp
        import numpy as np
        N_NODES = 50000
        N_EDGES = 12500
        D = 128
        N_LAYERS = 4
        BN_EPS = 1e-05
        key = jax.random.key(seed)
        ks = jax.random.split(key, 6)
        x = jax.random.normal(ks[0], (N_NODES, D), dtype=jnp.float32)
        src = jax.random.randint(ks[1], (N_EDGES,), 0, N_NODES, dtype=jnp.int32)
        dst = jax.random.randint(ks[2], (N_EDGES,), 0, N_NODES, dtype=jnp.int32)
        Ws = jax.random.normal(ks[3], (N_LAYERS, D, D), dtype=jnp.float32) * 0.05
        bs = jnp.zeros((N_LAYERS, D), dtype=jnp.float32)
        gammas = jnp.ones((N_LAYERS, D), dtype=jnp.float32)
        betas = jnp.zeros((N_LAYERS, D), dtype=jnp.float32)
        lin1_w = jax.random.normal(ks[4], (D, D), dtype=jnp.float32) * 0.05
        lin1_b = jnp.zeros((D,), dtype=jnp.float32)
        return {'x': x, 'src': src, 'dst': dst, 'Ws': Ws, 'bs': bs, 'gammas': gammas, 'betas': betas, 'lin1_w': lin1_w, 'lin1_b': lin1_b}
    _L2_gnn_all = _L2_gnn_setup()
    _L2_gnn_in = {k: v for k, v in _L2_gnn_all.items() if k in ('Ws', 'bs', 'gammas', 'betas', 'lin1_w', 'lin1_b')}
    del _L2_gnn_all

    def _L3_gnn_setup():
        import jax, jax.numpy as jnp
        import numpy as np
        N_NODES = 625
        N_EDGES = 10000
        IN_DIM, HID_DIM, OUT_DIM = (128, 256, 128)
        key = jax.random.key(seed)
        ks = jax.random.split(key, 8)
        x = jax.random.normal(ks[0], (N_NODES, IN_DIM), dtype=jnp.float32)
        edge_index = jax.random.randint(ks[1], (2, N_EDGES), 0, N_NODES, dtype=jnp.int64)

        def glorot(k, fan_in, fan_out):
            lim = 1.0 / np.sqrt(fan_in)
            return jax.random.uniform(k, (fan_in, fan_out), dtype=jnp.float32, minval=-lim, maxval=lim)
        W0 = glorot(ks[2], IN_DIM, HID_DIM)
        W1 = glorot(ks[3], HID_DIM, HID_DIM)
        W2 = glorot(ks[4], HID_DIM, OUT_DIM)
        b0 = jnp.zeros((HID_DIM,), dtype=jnp.float32)
        b1 = jnp.zeros((HID_DIM,), dtype=jnp.float32)
        b2 = jnp.zeros((OUT_DIM,), dtype=jnp.float32)
        return {'x': x, 'edge_index': edge_index, 'W0': W0, 'b0': b0, 'W1': W1, 'b1': b1, 'W2': W2, 'b2': b2}
    _L3_gnn_all = _L3_gnn_setup()
    _L3_gnn_in = {k: v for k, v in _L3_gnn_all.items() if k in ('W0', 'b0', 'W1', 'b1', 'W2', 'b2')}
    del _L3_gnn_all
    return {'x': x, 'src': src, 'dst': dst, 'L0_gnn_Ws0': _L0_gnn_in['Ws0'], 'L0_gnn_Wn0': _L0_gnn_in['Wn0'], 'L0_gnn_b0': _L0_gnn_in['b0'], 'L0_gnn_Ws1': _L0_gnn_in['Ws1'], 'L0_gnn_Wn1': _L0_gnn_in['Wn1'], 'L0_gnn_b1': _L0_gnn_in['b1'], 'L0_gnn_Ws2': _L0_gnn_in['Ws2'], 'L0_gnn_Wn2': _L0_gnn_in['Wn2'], 'L0_gnn_b2': _L0_gnn_in['b2'], 'L1_gnn_W1': _L1_gnn_in['W1'], 'L1_gnn_att_src1': _L1_gnn_in['att_src1'], 'L1_gnn_att_dst1': _L1_gnn_in['att_dst1'], 'L1_gnn_b1': _L1_gnn_in['b1'], 'L1_gnn_ln1_w': _L1_gnn_in['ln1_w'], 'L1_gnn_ln1_b': _L1_gnn_in['ln1_b'], 'L1_gnn_W2': _L1_gnn_in['W2'], 'L1_gnn_att_src2': _L1_gnn_in['att_src2'], 'L1_gnn_att_dst2': _L1_gnn_in['att_dst2'], 'L1_gnn_b2': _L1_gnn_in['b2'], 'L1_gnn_ln2_w': _L1_gnn_in['ln2_w'], 'L1_gnn_ln2_b': _L1_gnn_in['ln2_b'], 'L2_gnn_Ws': _L2_gnn_in['Ws'], 'L2_gnn_bs': _L2_gnn_in['bs'], 'L2_gnn_gammas': _L2_gnn_in['gammas'], 'L2_gnn_betas': _L2_gnn_in['betas'], 'L2_gnn_lin1_w': _L2_gnn_in['lin1_w'], 'L2_gnn_lin1_b': _L2_gnn_in['lin1_b'], 'L3_gnn_W0': _L3_gnn_in['W0'], 'L3_gnn_b0': _L3_gnn_in['b0'], 'L3_gnn_W1': _L3_gnn_in['W1'], 'L3_gnn_b1': _L3_gnn_in['b1'], 'L3_gnn_W2': _L3_gnn_in['W2'], 'L3_gnn_b2': _L3_gnn_in['b2']}

def reference(x, src, dst, L0_gnn_Ws0, L0_gnn_Wn0, L0_gnn_b0, L0_gnn_Ws1, L0_gnn_Wn1, L0_gnn_b1, L0_gnn_Ws2, L0_gnn_Wn2, L0_gnn_b2, L1_gnn_W1, L1_gnn_att_src1, L1_gnn_att_dst1, L1_gnn_b1, L1_gnn_ln1_w, L1_gnn_ln1_b, L1_gnn_W2, L1_gnn_att_src2, L1_gnn_att_dst2, L1_gnn_b2, L1_gnn_ln2_w, L1_gnn_ln2_b, L2_gnn_Ws, L2_gnn_bs, L2_gnn_gammas, L2_gnn_betas, L2_gnn_lin1_w, L2_gnn_lin1_b, L3_gnn_W0, L3_gnn_b0, L3_gnn_W1, L3_gnn_b1, L3_gnn_W2, L3_gnn_b2):
    import jax
    import jax.numpy as jnp

    def _L0_gnn_ref(x, src, dst, Ws0, Wn0, b0, Ws1, Wn1, b1, Ws2, Wn2, b2):
        import jax, jax.numpy as jnp
        import numpy as np
        N_NODES = 100000
        N_EDGES = 25000
        IN_F, HID_F, OUT_F = (128, 256, 128)
        N = x.shape[0]
        deg = jax.ops.segment_sum(jnp.ones_like(dst, dtype=x.dtype), dst, num_segments=N)
        deg = jnp.maximum(deg, 1.0)[:, None]

        def sage_layer(h, Ws, Wn, b):
            agg = jax.ops.segment_sum(h[src], dst, num_segments=N) / deg
            return jax.nn.relu(h @ Ws + agg @ Wn + b)
        h = sage_layer(x, Ws0, Wn0, b0)
        h = sage_layer(h, Ws1, Wn1, b1)
        h = sage_layer(h, Ws2, Wn2, b2)
        return h

    def _L1_gnn_ref(x, edge_index, W1, att_src1, att_dst1, b1, ln1_w, ln1_b, W2, att_src2, att_dst2, b2, ln2_w, ln2_b):
        import jax, jax.numpy as jnp
        import numpy as np
        N, E = (50000, 12500)
        IN_DIM, HC, OUT_DIM = (128, 64, 128)
        NEG_SLOPE = 0.2
        EPS = 1e-05

        def gat_conv(x, src, dst, W, att_src, att_dst, bias, heads, C, concat):
            n = x.shape[0]
            h = (x @ W).reshape(n, heads, C)
            a_src = jnp.einsum('nhc,hc->nh', h, att_src)
            a_dst = jnp.einsum('nhc,hc->nh', h, att_dst)
            e = jax.nn.leaky_relu(a_src[src] + a_dst[dst], NEG_SLOPE)
            emax = jax.ops.segment_max(e, dst, num_segments=n)
            ex = jnp.exp(e - emax[dst])
            denom = jax.ops.segment_sum(ex, dst, num_segments=n)
            alpha = ex / (denom[dst] + 1e-16)
            out = jax.ops.segment_sum(h[src] * alpha[:, :, None], dst, num_segments=n)
            out = out.reshape(n, heads * C) if concat else out.mean(axis=1)
            return out + bias

        def graph_layernorm(x, w, b):
            mean = x.mean()
            xc = x - mean
            var = (xc * xc).mean()
            return xc * jax.lax.rsqrt(var + EPS) * w + b
        n = x.shape[0]
        loop = jnp.arange(n, dtype=edge_index.dtype)
        src = jnp.concatenate([edge_index[0], loop])
        dst = jnp.concatenate([edge_index[1], loop])
        h = gat_conv(x, src, dst, W1, att_src1, att_dst1, b1, heads=2, C=HC, concat=True)
        h = jax.nn.relu(graph_layernorm(h, ln1_w, ln1_b))
        h = gat_conv(h, src, dst, W2, att_src2, att_dst2, b2, heads=1, C=OUT_DIM, concat=False)
        h = graph_layernorm(h, ln2_w, ln2_b)
        s0, d0 = (edge_index[0], edge_index[1])
        agg = jax.ops.segment_sum(h[s0], d0, num_segments=n)
        cnt = jax.ops.segment_sum(jnp.ones(s0.shape, h.dtype), d0, num_segments=n)
        mean_agg = agg / jnp.maximum(cnt, 1.0)[:, None]
        return jax.nn.relu(mean_agg + x)

    def _L2_gnn_ref(x, src, dst, Ws, bs, gammas, betas, lin1_w, lin1_b):
        import jax, jax.numpy as jnp
        import numpy as np
        N_NODES = 50000
        N_EDGES = 12500
        D = 128
        N_LAYERS = 4
        BN_EPS = 1e-05
        n = x.shape[0]
        ones = jnp.ones(src.shape[0], dtype=x.dtype)
        deg_out = jax.ops.segment_sum(ones, src, num_segments=n)
        deg_in = jax.ops.segment_sum(ones, dst, num_segments=n)
        norm_src = jax.lax.rsqrt(jnp.maximum(deg_out, 1.0))[:, None]
        norm_dst = jax.lax.rsqrt(jnp.maximum(deg_in, 1.0))[:, None]
        h = x
        xs = []
        for i in range(N_LAYERS):
            m = h * norm_src
            agg = jax.ops.segment_sum(m[src], dst, num_segments=n)
            h = agg * norm_dst
            h = jax.nn.relu(h @ Ws[i] + bs[i])
            mu = jnp.mean(h, axis=0)
            var = jnp.var(h, axis=0)
            h = (h - mu) * jax.lax.rsqrt(var + BN_EPS) * gammas[i] + betas[i]
            h = jax.nn.relu(h)
            xs.append(h)
        x_jk = jnp.max(jnp.stack(xs, axis=0), axis=0)
        out = jax.nn.relu(x_jk @ lin1_w + lin1_b)
        return out

    def _L3_gnn_ref(x, edge_index, W0, b0, W1, b1, W2, b2):
        import jax, jax.numpy as jnp
        import numpy as np
        N_NODES = 625
        N_EDGES = 10000
        IN_DIM, HID_DIM, OUT_DIM = (128, 256, 128)
        N = x.shape[0]
        loops = jnp.arange(N, dtype=edge_index.dtype)
        row = jnp.concatenate([edge_index[0], loops])
        col = jnp.concatenate([edge_index[1], loops])
        deg = jax.ops.segment_sum(jnp.ones(col.shape[0], dtype=x.dtype), col, num_segments=N)
        dinv = jnp.where(deg > 0, jax.lax.rsqrt(deg), 0.0)
        norm = (dinv[row] * dinv[col])[:, None]

        def gcn_layer(h, W, b):
            hW = h @ W
            msg = norm * hW[row]
            out = jax.ops.segment_sum(msg, col, num_segments=N)
            return out + b
        h = jax.nn.relu(gcn_layer(x, W0, b0))
        h = jax.nn.relu(gcn_layer(h, W1, b1))
        h = gcn_layer(h, W2, b2)
        return h
    edge_index = jnp.stack([src, dst])
    x = _layernorm(x + _L0_gnn_ref(x, src, dst, L0_gnn_Ws0, L0_gnn_Wn0, L0_gnn_b0, L0_gnn_Ws1, L0_gnn_Wn1, L0_gnn_b1, L0_gnn_Ws2, L0_gnn_Wn2, L0_gnn_b2), axis=-1)
    x = _layernorm(x + _L1_gnn_ref(x, edge_index, L1_gnn_W1, L1_gnn_att_src1, L1_gnn_att_dst1, L1_gnn_b1, L1_gnn_ln1_w, L1_gnn_ln1_b, L1_gnn_W2, L1_gnn_att_src2, L1_gnn_att_dst2, L1_gnn_b2, L1_gnn_ln2_w, L1_gnn_ln2_b), axis=-1)
    x = _layernorm(x + _L2_gnn_ref(x, src, dst, L2_gnn_Ws, L2_gnn_bs, L2_gnn_gammas, L2_gnn_betas, L2_gnn_lin1_w, L2_gnn_lin1_b), axis=-1)
    x = _layernorm(x + _L3_gnn_ref(x, edge_index, L3_gnn_W0, L3_gnn_b0, L3_gnn_W1, L3_gnn_b1, L3_gnn_W2, L3_gnn_b2), axis=-1)
    return x

_drawn_inputs = setup_inputs


def setup_inputs(seed=0):
    import zlib

    import numpy as np

    out = dict(_drawn_inputs(seed))
    spreads = {'L1_gnn_b1': (0.0, 0.423),
     'L1_gnn_ln1_w': (1.0, 0.2),
     'L1_gnn_ln1_b': (0.0, 0.451),
     'L1_gnn_b2': (0.0, 0.297),
     'L1_gnn_ln2_w': (1.0, 0.2),
     'L1_gnn_ln2_b': (0.0, 0.343),
     'L2_gnn_bs': (0.0, 0.1),
     'L2_gnn_gammas': (1.0, 0.2),
     'L2_gnn_betas': (0.0, 0.286),
     'L2_gnn_lin1_b': (0.0, 0.1),
     'L3_gnn_b0': (0.0, 0.505),
     'L3_gnn_b1': (0.0, 0.1),
     'L3_gnn_b2': (0.0, 0.1)}
    factors = {'L0_gnn_b0': 8.0,
     'L0_gnn_b1': 8.0,
     'L0_gnn_b2': 7.249,
     'L1_gnn_att_src1': 3.807,
     'L1_gnn_att_dst1': 57.057,
     'L1_gnn_att_src2': 12.598,
     'L1_gnn_att_dst2': 48.658}
    for name, (base, spread) in spreads.items():
        noise = np.random.default_rng([zlib.crc32(name.encode()), seed]).standard_normal(out[name].shape)
        drawn = base * np.exp(spread * noise) if base else spread * noise
        out[name] = jnp.asarray(drawn.astype(out[name].dtype))
    for name, factor in factors.items():
        out[name] = (out[name] * factor).astype(out[name].dtype)
    return out
```

```python
from contextlib import ExitStack

import concourse.bass as bass
from concourse import mybir

ALU = mybir.AluOpType
ACT = mybir.ActivationFunctionType
AX = mybir.AxisListType
F32 = mybir.dt.float32
BF16 = mybir.dt.bfloat16
I32 = mybir.dt.int32
U8 = mybir.dt.uint8

P = 128
SUB = 4
GROUP = SUB * P
N_NODES, N_EDGES, D, HID = 50000, 25000, 128, 256
NG = -(-N_NODES // GROUP)
EG = -(-N_EDGES // GROUP)
ET = EG * SUB
NODES_PAD = NG * GROUP
SLOTS = EG * GROUP
PAD_NODE = NODES_PAD - 1
NODE_TAIL = (N_NODES - (NG - 1) * GROUP) // SUB
RJ = 256
RQ = SLOTS // RJ
V_ROWS = SLOTS + NODES_PAD
BIG = 1e30
EPS = 1e-5
assert NODE_TAIL * SUB + (NG - 1) * GROUP == N_NODES and RQ * RJ == SLOTS


class Group:

    def __init__(self, i, off):
        if isinstance(i, int):
            i, off = 0, 2 * i + off
            self.number = off
        else:
            self.number = None
        self.i, self.off, self.b = i, off, off % 2

    def lag(self, k):
        return Group(self.i, self.off - k)

    def times(self, m, plus=0):
        if self.number is not None:
            return self.number * m + plus
        return self.i * (2 * m) + (self.off * m + plus)


class CountSem:

    def __init__(self, sem, per, n):
        self.sem, self.per, self.n = sem, per, n


class DmaSems:

    def __init__(self, sems, per, n):
        self.sems, self.per, self.n = sems, per, n

    def of(self, g):
        return self.sems[g.b]


def wait_for(eng, what, g, count=None):
    if g.number is not None:
        if g.number < 0:
            return
        if g.number >= what.n:
            g, count = Group(0, what.n - 1), None
    if isinstance(what, CountSem):
        eng.wait_ge(what.sem, g.times(what.per, what.per if count is None else count))
    elif g.number is not None:
        eng.wait_ge(what.sems[g.b], 16 * what.per * (g.number // 2 + 1))
    else:
        eng.wait_ge(what.sems[g.b], g.i * (16 * what.per) + 16 * what.per * (g.off // 2 + 1))


def wait_for_all(eng, what):
    for k in range(max(0, what.n - 2), what.n):
        wait_for(eng, what, Group(0, k))


def settle(ph, eng, g):
    if g.number is None:
        eng.sem_inc(ph.passed, 1)


def run_groups(eng, n, stages):
    low = min(lag for _, lag in stages)
    stages = [(f, lag - low) for f, lag in stages]
    most = max(lag for _, lag in stages)
    first = (most + 3) // 2 * 2

    def static(step):
        for f, lag in stages:
            if 0 <= step - lag < n:
                f(Group(0, step - lag))

    for step in range(first):
        static(step)
    with eng.Fori(first // 2, (n - 1) // 2) as i:
        for off in range(2):
            for f, lag in stages:
                f(Group(i, off).lag(lag))
    for step in range((n - 1) // 2 * 2, n + most):
        static(step)


class Phase:

    def __init__(self, nc, name, n):
        self.nc, self.name, self.n = nc, name, n
        self.ctx = ExitStack()
        self.sems = []
        self.passed = self.sem("passed")

    def sb(self, name, shape, dt=F32):
        return self.ctx.enter_context(self.nc.sbuf_tensor(f"{self.name}_{name}", shape, dt))

    def ps(self, name, shape, dt=F32):
        return self.ctx.enter_context(self.nc.psum_tensor(f"{self.name}_{name}", shape, dt))

    def sem(self, name):
        self.sems.append(self.nc.alloc_semaphore(f"{self.name}_{name}"))
        return self.sems[-1]

    def count_sem(self, name, per=1):
        return CountSem(self.sem(name), per, self.n)

    def dma_sems(self, name, per=1):
        return DmaSems([self.sem(f"{name}{b}") for b in range(2)], per, self.n)

    def block(self):
        return self.ctx.enter_context(self.nc.Block())

    def close(self):
        self.ctx.close()
        self.nc.clear_and_free_semaphores(self.sems)
        self.nc.all_engine_barrier()


def node_rows(table, first=0):
    return table[first:first + NODES_PAD].rearrange("(g p s) d -> g p s d", p=P, s=SUB)


def slot_rows(table, first=0):
    return table[first:first + SLOTS].rearrange("(g s p) d -> g p s d", p=P, s=SUB)


def at(view, g):
    if g.number is not None:
        return view[g.number]
    return view[g.times(1)]


def cols(g, width, plus=0, size=None):
    size = width if size is None else size
    if g.number is not None:
        return slice(g.number * width + plus, g.number * width + plus + size)
    return bass.ds(g.times(width, plus), size)



class Segments:

    def __init__(self, ph, K, jobs, flags=0):
        self.K, self.jobs, self.flags, self.n, self.rows_made = K, jobs, flags, 0, 0
        self.edge = ph.sb("edge", [RQ, 1])
        self.carry = ph.sb("carry", [1, RQ])
        self.row_ps = ph.ps("row_ps", [P, RQ])
        self.col_ps = ph.ps("col_ps", [P, 1])
        self.edge_ready, self.row_ready = ph.sem("edge_ready"), ph.sem("row_ready")
        self.carry_ready, self.col_ready = ph.sem("carry_ready"), ph.sem("col_ready")

    def tensor_side(self, pe, begin=0, end=None):
        K = self.K
        for n in range(1, self.flags + 1):
            pe.wait_ge(self.edge_ready, n)
            pe.transpose(self.row_ps[0:1, :], self.edge[:], K.ident[0:RQ, 0:RQ]).then_inc(self.row_ready, 1)
        for n in range(begin + 1, (self.jobs if end is None else end) + 1):
            pe.wait_ge(self.edge_ready, self.flags + n)
            pe.transpose(self.row_ps[0:1, :], self.edge[:], K.ident[0:RQ, 0:RQ]).then_inc(self.row_ready, 1)
            pe.wait_ge(self.carry_ready, n)
            pe.transpose(self.col_ps[0:RQ, :], self.carry[:], K.ident[0:1, 0:1]).then_inc(self.col_ready, 1)

    def flag_row(self, dve, link, row, column):
        self.rows_made += 1
        dve.tensor_copy(self.edge[:], column).then_inc(self.edge_ready, 1)
        dve.wait_ge(self.row_ready, self.rows_made)
        link(dve.tensor_copy(row, self.row_ps[0:1, :]))

    def across(self, dve, link, edge, coef, op0, op1, initial, backwards):
        self.n += 1
        link(dve.memset(self.carry[:], 0.0))
        dve.tensor_copy(self.edge[:], edge).then_inc(self.edge_ready, 1)
        dve.wait_ge(self.row_ready, self.flags + self.n)
        if backwards:
            out, k, v = self.carry[:, 0:RQ - 1], coef[0:1, 1:RQ], self.row_ps[0:1, 1:RQ]
            out, k, v = out[:, ::-1], k[:, ::-1], v[:, ::-1]
        else:
            out, k, v = self.carry[:, 1:RQ], coef[0:1, 0:RQ - 1], self.row_ps[0:1, 0:RQ - 1]
        dve.tensor_tensor_scan(out, k, v, initial, op0, op1).then_inc(self.carry_ready, 1)
        dve.wait_ge(self.col_ready, self.n)

    def running_sum(self, dve, link, out, v):
        K = self.K
        link(dve.tensor_tensor_scan(out, K.cont[:], v, 0.0, ALU.mult, ALU.add))
        self.across(dve, link, out[:, RJ - 1:RJ], K.whole_row, ALU.mult, ALU.add, 0.0, False)
        link(dve.scalar_tensor_tensor(out, K.first_seg[:], self.col_ps[0:RQ, :], out, ALU.mult, ALU.add))

    def running_max(self, dve, link, out, v):
        K = self.K
        link(dve.tensor_tensor_scan(out, K.cont_pen[:], v, -BIG, ALU.add, ALU.max))
        self.across(dve, link, out[:, RJ - 1:RJ], K.whole_pen_row, ALU.add, ALU.max, -BIG, False)
        link(dve.scalar_tensor_tensor(out, K.first_pen[:], self.col_ps[0:RQ, :], out, ALU.add, ALU.max))

    def spread_last(self, dve, link, out, v):
        K = self.K
        link(dve.tensor_tensor(out, v, K.last[:], ALU.mult))
        link(dve.tensor_tensor_scan(out[:, ::-1], K.notlast[:, ::-1], out[:, ::-1], 0.0, ALU.mult, ALU.add))
        self.across(dve, link, out[:, 0:1], K.open_row, ALU.mult, ALU.add, 0.0, True)
        link(dve.scalar_tensor_tensor(out, K.open_seg[:], self.col_ps[0:RQ, :], out, ALU.mult, ALU.add))


def linker(eng, sem):
    count = [0]

    def link(ins):
        count[0] += 1
        ins.then_inc(sem, 1)
        eng.wait_ge(sem, count[0])
    return link


class Constants:

    def __init__(self, nc, ctx):
        def sb(name, shape, dt=F32):
            return ctx.enter_context(nc.sbuf_tensor(name, shape, dt))
        self.ident = sb("ident", [P, P])
        self.ones = sb("ones", [P, P])
        R = [RQ, RJ]
        self.last, self.notlast, self.cont, self.cont_pen = (sb(n, R) for n in ("last", "notlast", "cont", "cont_pen"))
        self.real = sb("real", R)
        self.first_seg, self.first_pen, self.open_seg = (sb(n, R) for n in ("first_seg", "first_pen", "open_seg"))
        self.whole_row, self.whole_pen_row, self.open_row = (sb(n, [1, RQ]) for n in ("whole_row", "whole_pen_row", "open_row"))
        C = [P, ET]
        self.dst_c, self.src_c, self.src_hi, self.src_lo = (sb(n, C) for n in ("dst_c", "src_c", "src_hi", "src_lo"))
        self.dst_hi, self.dst_lo, self.last_c, self.inv_deg = (sb(n, C) for n in ("dst_hi", "dst_lo", "last_c", "inv_deg"))
        self.norm_dst, self.dinv = (sb(n, C) for n in ("norm_dst", "dinv"))
        self.src_x, self.dst_x, self.src_node, self.idx = (sb(n, C, I32) for n in ("src_x", "dst_x", "src_node", "idx"))
        self.idx_y, self.idx_jk, self.idx_out = (sb(n, C, I32) for n in ("idx_y", "idx_jk", "idx_out"))
        self.l2_weight = sb("l2_weight", C)
        self.dinv_last = sb("dinv_last", C)
        self.node_mask = sb("node_mask", [P, NG, SUB])

    def make_room(self, nc, ctx):
        def sb(name, shape, dt=F32):
            return ctx.enter_context(nc.sbuf_tensor(name, shape, dt))
        self.same = sb("same", [P, SLOTS], U8)
        self.goes_on = sb("goes_on", [P, SLOTS], U8)
        self.last_row = sb("last_row", [P, SLOTS], U8)
        self.att = sb("att", [P, ET, 4])
        self.alpha = sb("alpha", [P, 2, ET])
        self.alpha_self = sb("alpha_self", [P, 2, ET])



MATRICES = {
    "ws0": ("L0_gnn_Ws0", D, HID), "wn0": ("L0_gnn_Wn0", D, HID),
    "ws1": ("L0_gnn_Ws1", HID, HID), "wn1": ("L0_gnn_Wn1", HID, HID),
    "ws2": ("L0_gnn_Ws2", HID, D), "wn2": ("L0_gnn_Wn2", HID, D),
    "gat1": ("L1_gnn_W1", D, D), "gat2": ("L1_gnn_W2", D, D), "lin": ("L2_gnn_lin1_w", D, D),
    "gcn0": ("L3_gnn_W0", D, HID), "gcn1": ("L3_gnn_W1", HID, HID), "gcn2": ("L3_gnn_W2", HID, D),
}
ROW_VECTORS = {
    "b2": "L0_gnn_b2", "gat1_b": "L1_gnn_b1", "gat2_b": "L1_gnn_b2", "gcn2_b": "L3_gnn_b2",
}
COLUMN_VECTORS = {
    "b0_c": ("L0_gnn_b0", HID), "b1_c": ("L0_gnn_b1", HID), "gat1_b_c": ("L1_gnn_b1", D),
    "ln1_w_c": ("L1_gnn_ln1_w", D), "ln1_b_c": ("L1_gnn_ln1_b", D), "lin_b_c": ("L2_gnn_lin1_b", D),
    "gat2_b_c": ("L1_gnn_b2", D), "ln2_w_c": ("L1_gnn_ln2_w", D), "ln2_b_c": ("L1_gnn_ln2_b", D),
    "gcn0_b_c": ("L3_gnn_b0", HID), "gcn1_b_c": ("L3_gnn_b1", HID),
}
LAYERS = 4


class Weights:
    def __init__(self, nc, ctx):
        def sb(name, shape):
            return ctx.enter_context(nc.sbuf_tensor(f"w_{name}", shape, F32))
        beside = {"gat1": 4, "gat2": 2}
        self.wide = {k: sb(k, [P, rows // P, cols + beside.get(k, 0)])[:] for k, (_, rows, cols) in MATRICES.items()}
        self.m = {k: self.wide[k][:, :, 0:cols] for k, (_, _, cols) in MATRICES.items()}
        self.row = {k: sb(k, [P, D]) for k in ROW_VECTORS}
        self.col = {k: sb(k, [P, n // P]) for k, (_, n) in COLUMN_VECTORS.items()}
        self.jk_w = sb("jk_w", [P, LAYERS, D])
        self.jk_b, self.jk_gamma, self.jk_beta = (sb(n, [P, LAYERS]) for n in ("jk_b", "jk_gamma", "jk_beta"))
        self.att1, self.att2 = (self.wide[k][:, 0, D:D + n] for k, n in beside.items())
        self.eps = sb("eps", [P, 1])
        self.ln1_scale, self.ln1_shift = sb("ln1_scale", [P, 1]), sb("ln1_shift", [P, 1])
        self.ln2_scale, self.ln2_shift = sb("ln2_scale", [P, 1]), sb("ln2_shift", [P, 1])
        self.jk_scale, self.jk_shift, self.jk_const = (sb(n, [P, LAYERS]) for n in ("jk_scale", "jk_shift", "jk_const"))
        self.jk_scale_row, self.jk_shift_row = sb("jk_scale_row", [P, D]), sb("jk_shift_row", [P, D])
        self.lonely_row = sb("lonely_row", [P, D])


def setup_block(nc, A, K, W, tables):
    ph = Phase(nc, "setup", 0)
    R = [RQ, RJ]
    dst_i, src_i, next_i, hi_i, lo_i = (ph.sb(n, R, I32) for n in ("dst_i", "src_i", "next_i", "hi_i", "lo_i"))
    before_i = ph.sb("before_i", [RQ, 1], I32)
    before = ph.sb("before", [RQ, 1])
    minus_one = ph.sb("minus_one", [1, 1], I32)
    link_f = ph.sb("link_f", [RQ, 1])
    names = ("dst_r", "src_r", "next_r", "src_hi_r", "src_lo_r", "dst_hi_r", "dst_lo_r", "deg", "deg_1", "inv_r", "norm_r", "dinv_r")
    r = {n: ph.sb(n, R) for n in names}
    att1_in, att2_in = ph.sb("att1_in", [P, 4]), ph.sb("att2_in", [P, 2])
    w1_t, w2_t = ph.sb("w1_t", [P, P]), ph.sb("w2_t", [P, P])
    turn_ps = [ph.ps(f"turn{b}", [P, P]) for b in range(2)]
    att_ps = ph.ps("att_ps", [P, 8])
    edges_in, weights_in, pads_set = ph.sem("edges_in"), ph.sem("weights_in"), ph.sem("pads_set")
    out_done = ph.sem("out_done")
    ident_ready, chain, achain = ph.sem("ident_ready"), ph.sem("chain"), ph.sem("achain")
    deg_ready, roots_ready, turn_ready, turned, turn_read = (ph.sem(n) for n in ("deg_ready", "roots_ready", "turn_ready", "turned", "turn_read"))
    att_t, att_read, att_out = ph.sem("att_t"), ph.sem("att_read"), ph.sem("att_out")
    seg = Segments(ph, K, 2, flags=3)
    full = (N_EDGES // RJ) * RJ
    rest = N_EDGES - full
    turns = [("dst_r", K.dst_c), ("src_r", K.src_c), ("src_hi_r", K.src_hi), ("src_lo_r", K.src_lo),
             ("dst_hi_r", K.dst_hi), ("dst_lo_r", K.dst_lo), (None, K.last_c),
             ("inv_r", K.inv_deg), ("norm_r", K.norm_dst), ("dinv_r", K.dinv)]
    edge_loads = 8
    column = "one column to a partition, once"
    block = ph.block()

    @block.sync
    def _(sp):
        sp.wait_ge(pads_set, 6)
        def rows(tile, vec, off):
            n = (N_EDGES - off - full)
            sp.dma_start(tile[0:RQ - 1, :], vec[off:off + full].rearrange("(q j) -> q j", j=RJ)).then_inc(edges_in, 16)
            sp.dma_start(tile[RQ - 1:RQ, 0:n], vec[off + full:N_EDGES].rearrange("(a j) -> a j", a=1)).then_inc(edges_in, 16)
        rows(dst_i, A["dst"], 0)
        rows(src_i, A["src"], 0)
        rows(next_i, A["dst"], 1)
        with nc.allow_non_contiguous_dma(reason=column):
            ends = A["dst"][RJ - 1:RJ - 1 + full - RJ].rearrange("(q j) -> q j", j=RJ)[:, 0:1]
            sp.dma_start(before_i[1:RQ - 1, :], ends).then_inc(edges_in, 16)
            sp.dma_start(before_i[RQ - 1:RQ, :], A["dst"][full - 1:full].rearrange("(a j) -> a j", a=1)).then_inc(edges_in, 16)
            n = 0
            for k, (name, rows_, cols_) in MATRICES.items():
                sp.dma_start(W.m[k][:], A[name].rearrange("(c p) n -> p c n", p=P)).then_inc(weights_in, 16)
            for k, name in ROW_VECTORS.items():
                sp.dma_start(W.row[k][:], A[name].partition_broadcast(P)).then_inc(weights_in, 16)
            for k, (name, size) in COLUMN_VECTORS.items():
                sp.dma_start(W.col[k][:], A[name].rearrange("(c p) -> p c", p=P)).then_inc(weights_in, 16)
            sp.dma_start(W.jk_w[:], A["L2_gnn_Ws"].rearrange("l p n -> p l n")).then_inc(weights_in, 16)
            for tile, name in ((W.jk_b, "L2_gnn_bs"), (W.jk_gamma, "L2_gnn_gammas"), (W.jk_beta, "L2_gnn_betas")):
                sp.dma_start(tile[:], A[name].rearrange("l p -> p l")).then_inc(weights_in, 16)
            half = D // 2
            for c, name in enumerate(("L1_gnn_att_src1", "L1_gnn_att_dst1")):
                for h in range(2):
                    sp.dma_start(att1_in[h * half:(h + 1) * half, 2 * c + h:2 * c + h + 1],
                                 A[name][h:h + 1].rearrange("a p -> p a")).then_inc(weights_in, 16)
            for c, name in enumerate(("L1_gnn_att_src2", "L1_gnn_att_dst2")):
                sp.dma_start(att2_in[:, c:c + 1], A[name].rearrange("a p -> p a")).then_inc(weights_in, 16)
        sp.wait_ge(edges_in, 16 * edge_loads)
        sp.dma_start(tables["dst"][0:1].rearrange("(a j) -> a j", a=1), minus_one[:]).then_inc(out_done, 16)
        sp.dma_start(tables["dst"][1:1 + SLOTS].rearrange("(q j) -> q j", j=RJ), dst_i[:]).then_inc(out_done, 16)
        sp.dma_start(tables["dst"][1 + SLOTS:2 + SLOTS].rearrange("(a j) -> a j", a=1), dst_i[RQ - 1:RQ, RJ - 1:RJ]).then_inc(out_done, 16)
        sp.wait_ge(out_done, 48)
    weight_loads = len(MATRICES) + len(ROW_VECTORS) + len(COLUMN_VECTORS) + 4 + 6

    @block.gpsimd
    def _(pool):
        link = linker(pool, achain)
        for tile in (dst_i, src_i, next_i):
            pool.memset(tile[:], PAD_NODE).then_inc(pads_set, 1)
        pool.memset(before_i[:], -1).then_inc(pads_set, 1)
        pool.memset(att1_in[:], 0.0).then_inc(pads_set, 1)
        pool.memset(minus_one[:], -1).then_inc(pads_set, 1)
        link(pool.memset(K.ident[:], 0.0))
        pool.memset(K.ones[:], 1.0)
        pool.memset(W.eps[:], EPS)
        pool.affine_select(out=K.ident[:], in_=K.ident[:], compare_op=ALU.not_equal, fill=1.0, base=0,
                           pattern=[[-1, P]], channel_multiplier=1).then_inc(ident_ready, 1)

    @block.tensor
    def _(pe):
        pe.wait_ge(ident_ready, 1)
        seg.tensor_side(pe)
        pe.wait_ge(roots_ready, 1)
        n = 0
        for name, _c in turns:
            tile = K.last if name is None else r[name]
            for h in range(2):
                if n >= 2:
                    pe.wait_ge(turn_read, n - 1)
                pe.transpose(turn_ps[n % 2][:, 0:RQ], tile[:, h * P:(h + 1) * P], K.ident[0:RQ, 0:RQ]).then_inc(turned, 1)
                n += 1
        pe.wait_ge(turn_read, n)
        pe.wait_ge(weights_in, 16 * weight_loads)
        for b, name in enumerate(("gat1", "gat2")):
            pe.transpose(turn_ps[b][:], W.m[name][:, 0, :], K.ident[:]).then_inc(att_t, 1)
        pe.wait_ge(att_read, 2)
        pe.matmul(att_ps[:, 0:4], w1_t[:], att1_in[:], start=True, stop=True)
        pe.matmul(att_ps[:, 4:6], w2_t[:], att2_in[:], start=True, stop=True).then_inc(att_out, 1)

    @block.scalar
    def _(act):
        act.wait_ge(deg_ready, 1)
        act.activation(r["norm_r"][:], r["deg"][:], ACT.Sqrt).then_inc(turn_ready, 1)
        act.activation(r["dinv_r"][:], r["deg_1"][:], ACT.Sqrt).then_inc(turn_ready, 1)

    @block.vector
    def _(dve):
        link = linker(dve, chain)
        dve.wait_ge(edges_in, 16 * edge_loads)
        for name, tile in (("dst_r", dst_i), ("src_r", src_i), ("next_r", next_i)):
            dve.tensor_copy(r[name][:], tile[:])
        link(dve.tensor_copy(before[:], before_i[:]))
        for who, tile in (("src", src_i), ("dst", dst_i)):
            dve.tensor_single_scalar(hi_i[:], tile[:], 9, op=ALU.logical_shift_right)
            link(dve.tensor_single_scalar(lo_i[:], tile[:], GROUP - 1, op=ALU.bitwise_and))
            dve.tensor_copy(r[who + "_hi_r"][:], hi_i[:])
            link(dve.tensor_copy(r[who + "_lo_r"][:], lo_i[:]))
        dst = r["dst_r"]
        dve.tensor_scalar(K.real[:], dst[:], float(N_NODES), None, ALU.is_lt)
        dve.tensor_tensor(K.last[:], r["next_r"][:], dst[:], ALU.not_equal)
        dve.tensor_tensor(K.notlast[:], r["next_r"][:], dst[:], ALU.is_equal)
        dve.memset(K.cont[:, 0:1], 0.0)
        dve.tensor_tensor(K.cont[:, 1:RJ], dst[:, 1:RJ], dst[:, 0:RJ - 1], ALU.is_equal)
        link(dve.tensor_tensor(link_f[:], dst[:, 0:1], before[:], ALU.is_equal))
        dve.tensor_scalar(K.cont_pen[:], K.cont[:], 1.0, BIG, ALU.subtract, ALU.mult)
        dve.tensor_scalar(K.first_seg[:], dst[:], dst[:, 0:1], link_f[:], ALU.is_equal, ALU.mult)
        link(dve.tensor_scalar(K.open_seg[:], dst[:], dst[:, RJ - 1:RJ], K.notlast[:, RJ - 1:RJ], ALU.is_equal, ALU.mult))
        link(dve.tensor_scalar(K.first_pen[:], K.first_seg[:], 1.0, BIG, ALU.subtract, ALU.mult))
        dve.wait_ge(ident_ready, 1)
        flags = ((K.first_seg[:, RJ - 1:RJ], K.whole_row), (K.first_pen[:, RJ - 1:RJ], K.whole_pen_row), (K.open_seg[:, 0:1], K.open_row))
        for column_, row in flags:
            seg.flag_row(dve, link, row[:], column_)
        deg = r["deg"]
        link(dve.memset(r["inv_r"][:], 1.0))
        seg.running_sum(dve, link, deg[:], r["inv_r"][:])
        seg.spread_last(dve, link, deg[:], deg[:])
        link(dve.tensor_scalar(deg[:], deg[:], 1.0, None, ALU.max))
        link(dve.tensor_scalar(r["deg_1"][:], deg[:], 1.0, None, ALU.add))
        dve.sem_inc(deg_ready, 1)
        dve.wait_ge(turn_ready, 2)
        dve.reciprocal(r["inv_r"][:], deg[:])
        dve.reciprocal(r["norm_r"][:], r["norm_r"][:])
        dve.reciprocal(r["dinv_r"][:], r["dinv_r"][:]).then_inc(roots_ready, 1)
        n = 0
        for name, c in turns:
            for h in range(2):
                dve.wait_ge(turned, n + 1)
                dve.tensor_copy(c[:, h::2], turn_ps[n % 2][:, 0:RQ]).then_inc(turn_read, 1)
                n += 1
        dve.wait_ge(turn_read, n)
        dve.tensor_copy(K.src_node[:], K.src_c[:])
        dve.tensor_scalar(K.src_x[:], K.src_c[:], float(N_NODES - 1), None, ALU.min)
        dve.tensor_scalar(K.dst_x[:], K.dst_c[:], float(N_NODES - 1), None, ALU.min)
        dve.tensor_tensor(K.dinv_last[:], K.dinv[:], K.last_c[:], ALU.mult)
        link(dve.tensor_scalar(K.l2_weight[:], K.last_c[:], -65536.0, 65536.0, ALU.mult, ALU.add))
        link(dve.tensor_tensor(K.idx_out[:], K.l2_weight[:], K.dst_c[:], ALU.add))
        for b, tile in enumerate((w1_t, w2_t)):
            dve.wait_ge(att_t, b + 1)
            dve.tensor_copy(tile[:], turn_ps[b][:]).then_inc(att_read, 1)
        dve.wait_ge(att_out, 1)
        dve.tensor_copy(W.att1[:], att_ps[:, 0:4])
        link(dve.tensor_copy(W.att2[:], att_ps[:, 4:6]))

    ph.close()



def maps_block(nc, K, tables):
    ph = Phase(nc, "maps", EG)
    near = ph.sb("near", [P, 2, GROUP + 2], I32)
    iota_i = ph.sb("iota_i", [P, GROUP], I32)
    lo_iota, hi_iota = ph.sb("lo_iota", [P, GROUP], BF16), ph.sb("hi_iota", [P, P], BF16)
    node, slot1, has = (ph.sb(n, [P, GROUP]) for n in ("node", "slot1", "has"))
    tile_no, place_no = ph.sb("tile_no", [P, ET]), ph.sb("place_no", [P, ET])
    meta = ph.sb("meta", [P, GROUP, 2])
    lo_hot = ph.sb("lo_hot", [P, 2, 2, GROUP], BF16)
    hi_hot = ph.sb("hi_hot", [P, 2, 3, P], BF16)
    out_ps, tile_ps, place_ps = (ph.ps(n, [P, GROUP]) for n in ("out_ps", "tile_ps", "place_ps"))
    turn_ps = [ph.ps(f"turn{b}", [P, P]) for b in range(2)]
    near_in = ph.dma_sems("near_in")
    near_used, hot_ready, hot_used = ph.count_sem("near_used"), ph.count_sem("hot_ready", SUB), ph.count_sem("hot_used", SUB)
    iotas, chain, pchain, mask_ready, turned, meta_out, meta_ready = (ph.sem(n) for n in ("iotas", "chain", "pchain", "mask_ready", "turned", "meta_out", "meta_ready"))
    block = ph.block()

    @block.sync
    def _(sp):
        def load(g):
            wait_for(sp, near_used, g.lag(2))
            sp.dma_start(near[:, g.b, :], tables["dst"][cols(g, GROUP, 0, GROUP + 2)].partition_broadcast(P)).then_inc(near_in.of(g), 16)
        run_groups(sp, EG, [(load, 0)])
        sp.wait_ge(meta_ready, 1)
        sp.dma_start(tables["meta"].rearrange("(q c) k -> q c k", c=GROUP), meta[0:NG, :, :]).then_inc(meta_out, 16)
        sp.wait_ge(meta_out, 16)

    @block.gpsimd
    def _(pool):
        link = linker(pool, pchain)
        link(pool.iota(iota_i[:], pattern=[[1, GROUP]], base=-RJ, channel_multiplier=0))
        link(pool.tensor_copy(lo_iota[:], iota_i[:]))
        link(pool.iota(iota_i[:, 0:P], pattern=[[1, P]], base=0, channel_multiplier=0))
        link(pool.tensor_copy(hi_iota[:], iota_i[:, 0:P]))
        link(pool.iota(iota_i[:, 0:ET], pattern=[[1, ET]], base=1, channel_multiplier=0))
        link(pool.tensor_copy(tile_no[:], iota_i[:, 0:ET]))
        link(pool.iota(iota_i[:, 0:ET], pattern=[[0, ET]], base=0, channel_multiplier=1))
        link(pool.tensor_copy(place_no[:], iota_i[:, 0:ET]))
        link(pool.iota(iota_i[:], pattern=[[1, GROUP]], base=0, channel_multiplier=GROUP))
        pool.tensor_copy(node[:], iota_i[:]).then_inc(iotas, 1)

    @block.tensor
    def _(pe):
        def count(g):
            for s in range(SUB):
                wait_for(pe, hot_ready, g, s + 1)
                first, last = g.number == 0 and s == 0, g.number == EG - 1 and s == SUB - 1
                for h, (ps, side) in enumerate(((out_ps, 0), (tile_ps, 1), (place_ps, 1))):
                    mm = pe.matmul(ps[:], hi_hot[:, s % 2, h, :], lo_hot[:, s % 2, side, :], start=first, stop=last)
                mm.then_inc(hot_used.sem, 1)
        run_groups(pe, EG, [(count, 0)])
        for s in range(SUB):
            pe.wait_ge(mask_ready, s + 1)
            pe.transpose(turn_ps[s % 2][:, 0:NG], has[0:NG, s::SUB], K.ident[0:NG, 0:NG]).then_inc(turned, 1)

    @block.vector
    def _(dve):
        link = linker(dve, chain)
        dve.wait_ge(iotas, 1)
        dve.tensor_scalar(K.src_lo[:], K.src_lo[:], -float(RJ), None, ALU.add)
        dve.tensor_scalar(K.dst_lo[:], K.dst_lo[:], -float(RJ), None, ALU.add)
        dve.tensor_tensor(tile_no[:], tile_no[:], K.last_c[:], ALU.mult)
        link(dve.tensor_tensor(place_no[:], place_no[:], K.last_c[:], ALU.mult))

        def masks(g):
            wait_for(dve, near_in, g)
            now = near[:, g.b, :]
            dve.tensor_tensor(K.last_row[:, cols(g, GROUP)], now[:, 1:GROUP + 1], now[:, 2:GROUP + 2], ALU.not_equal)
            for s in range(SUB):
                tile = now[:, 1 + s * P:1 + (s + 1) * P]
                dve.tensor_scalar(K.same[:, cols(g, GROUP, s * P, P)], tile, K.dst_c[:, cols(g, SUB, s, 1)], None, ALU.is_equal)
                mm = dve.tensor_scalar(K.goes_on[:, cols(g, GROUP, s * P, P)], tile, now[:, s * P:s * P + 1], None, ALU.is_equal)
            mm.then_inc(near_used.sem, 1)

        def hots(g):
            for s in range(SUB):
                if s < 2:
                    wait_for(dve, hot_used, g.lag(1), s + 3)
                else:
                    wait_for(dve, hot_used, g, s - 1)
                t = cols(g, SUB, s, 1)
                dve.tensor_scalar(lo_hot[:, s % 2, 0, :], lo_iota[:], K.src_lo[:, t], None, ALU.is_equal)
                dve.tensor_scalar(lo_hot[:, s % 2, 1, :], lo_iota[:], K.dst_lo[:, t], None, ALU.is_equal)
                dve.tensor_scalar(hi_hot[:, s % 2, 0, :], hi_iota[:], K.src_hi[:, t], None, ALU.is_equal)
                dve.tensor_scalar(hi_hot[:, s % 2, 1, :], hi_iota[:], K.dst_hi[:, t], tile_no[:, t], ALU.is_equal, ALU.mult)
                dve.tensor_scalar(hi_hot[:, s % 2, 2, :], hi_iota[:], K.dst_hi[:, t], place_no[:, t], ALU.is_equal, ALU.mult).then_inc(hot_ready.sem, 1)
        run_groups(dve, EG, [(masks, 0), (hots, 0)])
        wait_for(dve, hot_used, Group(0, EG - 1))
        dve.tensor_copy(meta[:, :, 0], out_ps[:])
        dve.tensor_scalar(has[:], tile_ps[:], 1.0, None, ALU.min)
        link(dve.tensor_scalar(slot1[:], tile_ps[:], float(P), -float(P + SLOTS), ALU.mult, ALU.add))
        link(dve.tensor_tensor(slot1[:], slot1[:], place_ps[:], ALU.add))
        link(dve.tensor_tensor(slot1[:], slot1[:], node[:], ALU.subtract))
        link(dve.tensor_tensor(slot1[:], slot1[:], has[:], ALU.mult))
        link(dve.tensor_tensor(slot1[:], slot1[:], node[:], ALU.add))
        link(dve.tensor_scalar(meta[:, :, 1], slot1[:], float(SLOTS), None, ALU.add))
        dve.sem_inc(meta_ready, 1)
        link(dve.tensor_scalar(has[:], has[:], -1.0, 1.0, ALU.mult, ALU.add))
        link(dve.tensor_scalar(node[:], node[:], float(N_NODES), None, ALU.is_lt))
        link(dve.tensor_tensor(has[:], has[:], node[:], ALU.mult))
        dve.sem_inc(mask_ready, 2)
        for s in range(SUB):
            dve.wait_ge(turned, s + 1)
            dve.tensor_copy(K.node_mask[:, :, s], turn_ps[s % 2][:, 0:NG]).then_inc(mask_ready, 1)
    ph.close()


def pool_gather(pool, ph, g, index_tile, ring, ring_ready, used, table, into, arrived):
    by_tile = isinstance(used, CountSem) and used.per == SUB
    wait_for(pool, arrived if by_tile else used, g.lag(2))
    settle(ph, pool, g)
    pool.tensor_copy(ring[:, g.b, :], index_tile[:, cols(g, SUB)]).then_inc(ring_ready.sem, 1)
    wait_for(pool, ring_ready, g)
    settle(ph, pool, g)
    for s in range(SUB):
        if by_tile and s % 2 == 0:
            wait_for(pool, used, g.lag(2), s + 2)
            settle(ph, pool, g)
        pool.indirect_dma_start(out=into[:, g.b, s, :], out_offset=None, in_=table,
                                in_offset=bass.IndirectOffsetOnAxis(ap=ring[:, g.b, s:s + 1], axis=0)).then_inc(arrived.of(g), 16)


class SmallGather:

    def __init__(self, ph, table, width, index_tile, result):
        self.ph, self.table, self.index, self.result = ph, table, index_tile, result
        self.rows = ph.sb("small_rows", [P, 2, SUB, width])
        self.ring = ph.sb("small_ring", [P, 2, SUB], I32)
        self.ring_ready, self.used, self.arrived = ph.count_sem("small_ring_ready"), ph.count_sem("small_used"), ph.dma_sems("small_arrived", SUB)

    def pool_fetch(self, pool, g):
        pool_gather(pool, self.ph, g, self.index, self.ring, self.ring_ready, self.used, self.table, self.rows, self.arrived)

    def vector_keep(self, dve, g):
        wait_for(dve, self.arrived, g)
        settle(self.ph, dve, g)
        dve.tensor_copy(self.result[:, cols(g, SUB), :], self.rows[:, g.b, :, :]).then_inc(self.used.sem, 1)


def scores_block(nc, name, K, table, result):
    ph = Phase(nc, name, EG)
    small = SmallGather(ph, table, 2, K.idx, result)
    block = ph.block()

    @block.gpsimd
    def _(pool):
        run_groups(pool, EG, [(lambda g: small.pool_fetch(pool, g), 0)])

    @block.vector
    def _(dve):
        run_groups(dve, EG, [(lambda g: small.vector_keep(dve, g), 0)])
    ph.close()


def meta_block(nc, K, src_meta):
    with nc.sbuf_tensor("nodes_way", [P, ET], F32) as way:
        ph = Phase(nc, "meta", 0)
        chain, to_root, root = ph.sem("chain"), ph.sem("to_root"), ph.sem("root")
        block = ph.block()

        @block.scalar
        def _(act):
            act.wait_ge(to_root, 1)
            act.activation(K.l2_weight[:], K.l2_weight[:], ACT.Sqrt).then_inc(root, 1)

        @block.vector
        def _(dve):
            link = linker(dve, chain)
            where = src_meta[:, :, 1]
            link(dve.tensor_scalar(K.l2_weight[:], src_meta[:, :, 0], 1.0, None, ALU.max))
            dve.sem_inc(to_root, 1)
            link(dve.tensor_copy(K.idx[:], where))
            link(dve.tensor_scalar(way[:], where, float(SLOTS), float(V_ROWS), ALU.is_lt, ALU.mult))
            dve.tensor_tensor(K.idx_y[:], way[:], where, ALU.add)
            dve.tensor_scalar(K.idx_jk[:], where, float(SLOTS), None, ALU.min)
            dve.wait_ge(root, 1)
            link(dve.reciprocal(K.l2_weight[:], K.l2_weight[:]))
            link(dve.tensor_tensor(K.l2_weight[:], K.l2_weight[:], K.norm_dst[:], ALU.mult))
        ph.close()



def to_subs(row):
    return row[:].unsqueeze(1).broadcast_to([P, SUB, D])


class Norm:

    def __init__(self, ph, name):
        self.ph = ph
        self.stats, self.moments, self.root = (ph.sb(f"{name}_{n}", [P, 2, SUB, w]) for n, w in (("stats", 6), ("moments", 2), ("root", 1)))
        self.has_stats, self.has_moments, self.has_root, self.has_inverse, self.done = (
            ph.count_sem(f"{name}_{n}") for n in ("has_stats", "has_moments", "has_root", "has_inverse", "done"))

    def vector_moments(self, dve, g, rows):
        wait_for(dve, self.has_root, g.lag(2))
        for s in range(SUB):
            ins = dve.bn_stats(self.stats[:, g.b, s, :], rows[:, g.b, s, :])
        ins.then_inc(self.has_stats.sem, 1)
        wait_for(dve, self.has_stats, g)
        settle(self.ph, dve, g)
        for s in range(SUB):
            ins = dve.bn_aggr(self.moments[:, g.b, s, :], self.stats[:, g.b, s, :])
        ins.then_inc(self.has_moments.sem, 1)

    def scalar_root(self, act, g, eps):
        wait_for(act, self.has_moments, g)
        wait_for(act, self.done, g.lag(2))
        act.activation(self.root[:, g.b, :, 0], self.moments[:, g.b, :, 1], ACT.Sqrt, bias=eps[:]).then_inc(self.has_root.sem, 1)

    def vector_apply(self, dve, g, rows, out):
        wait_for(dve, self.has_root, g)
        dve.reciprocal(self.root[:, g.b, :, 0], self.root[:, g.b, :, 0]).then_inc(self.has_inverse.sem, 1)
        wait_for(dve, self.has_inverse, g)
        for s in range(SUB):
            ins = dve.tensor_scalar(out[:, g.b, s, :], rows[:, g.b, s, :], self.moments[:, g.b, s, 0:1],
                                    self.root[:, g.b, s, 0:1], ALU.subtract, ALU.mult)
        ins.then_inc(self.done.sem, 1)


def turn_rows(pe, ps, rows, ident):
    for s in range(SUB):
        mm = pe.transpose(ps[:, s * P:(s + 1) * P], rows[:, s, :], ident[:])
    return mm


def turn_back(pe, ps, feats, subs, ident):
    for n, s in enumerate(subs):
        for c in range(feats.shape[1]):
            mm = pe.transpose(ps[:, n, c * P:(c + 1) * P], feats[:, c, s * P:(s + 1) * P], ident[:])
    return mm


def layer_t(pe, ps, parts):
    terms = [(w, k, x) for w, x in parts for k in range(x.shape[1])]
    for c in range(ps.shape[1]):
        for n, (w, k, x) in enumerate(terms):
            mm = pe.matmul(ps[:, c, :], w[:, k, c * P:(c + 1) * P], x[:, k, :], start=n == 0, stop=n == len(terms) - 1)
    return mm


def layer_rows(pe, ps, parts):
    terms = [(w, k, x) for w, x in parts for k in range(x.shape[1])]
    for s in range(SUB):
        for n, (w, k, x) in enumerate(terms):
            mm = pe.matmul(ps[:, s, :], x[:, k, s * P:(s + 1) * P], w[:, k, :], start=n == 0, stop=n == len(terms) - 1)
    return mm


def lanes(bank, width):
    return bank[:].rearrange("p (s d) -> p s d", d=width)



def node_net_block(nc, name, K, W, tables, x, out):
    sage = name == "sage"
    ph = Phase(nc, f"{name}_nodes", NG)
    w0, w1, w2 = (W.m[n] for n in (("ws0", "ws1", "ws2") if sage else ("gcn0", "gcn1", "gcn2")))
    b0, b1 = (W.col[n] for n in (("b0_c", "b1_c") if sage else ("gcn0_b_c", "gcn1_b_c")))
    b2 = W.row["b2" if sage else "gcn2_b"]
    L = 0 if sage else 1
    rows4 = [P, 2, SUB, D]
    x_in, x_again, y, z = (ph.sb(n, rows4) for n in ("x_in", "x_again", "y", "z"))
    x_t = ph.sb("x_t", [P, 2, 1, GROUP])
    h1_t, h2_t = ph.sb("h1_t", [P, 2, 2, GROUP]), ph.sb("h2_t", [P, 2, 2, GROUP])
    h1, h2 = ph.sb("h1", [P, 2, SUB, HID]), ph.sb("h2", [P, 2, SUB, HID])
    bank_x, bank_y = ph.ps("bank_x", [P, GROUP]), ph.ps("bank_y", [P, GROUP])
    h1_ps, h2_ps = ph.ps("h1_ps", [P, 2, GROUP]), ph.ps("h2_ps", [P, 2, GROUP])
    ring = ph.ps("ring", [P, SUB, HID])
    norm = Norm(ph, "norm")
    x_loaded, x_reloaded = ph.dma_sems("x_loaded"), ph.dma_sems("x_reloaded")
    h1_stored, h2_stored, y_stored = ph.dma_sems("h1_stored"), ph.dma_sems("h2_stored"), ph.dma_sems("y_stored")
    S = ph.count_sem
    turned, x_copied, h1_made, h1_kept, h2_made, h2_kept = (S(n) for n in ("turned", "x_copied", "h1_made", "h1_kept", "h2_made", "h2_kept"))
    h1_turned, h1_out, h2_turned, h2_out = (S(n) for n in ("h1_turned", "h1_out", "h2_turned", "h2_out"))
    y_made, y_biased, y_summed = S("y_made"), S("y_biased"), S("y_summed")
    if sage:
        norm2 = Norm(ph, "norm2")
        x1_t, u, att = ph.sb("x1_t", [P, 2, 1, GROUP]), ph.sb("u", [P, 2, SUB, D + 2]), ph.sb("att", [P, 2, SUB, 2])
        x2 = ph.sb("x2", rows4)
        x1_turned, x1_copied, u_made, u_out, att_out, z_summed = (S(n) for n in ("x1_turned", "x1_copied", "u_made", "u_out", "att_out", "z_summed"))
        u_stored, att_stored = ph.dma_sems("u_stored"), ph.dma_sems("att_stored")
        u_biased, u_counted = S("u_biased"), S("u_counted")
        ub = ph.sb("ub", rows4)
        fetched, rings = ([ph.sb(f"{k}{n}", *shape) for n in range(2)] for k, shape in (("fetched", (rows4,)), ("fetch_ring", ([P, 2, SUB], I32))))
        ring_ready = [CountSem(ph.sem(f"ring_ready{n}"), 1, EG) for n in range(2)]
        fetch_done, stashed = ([DmaSems([ph.sem(f"{k}{n}_{b}") for b in range(2)], per, EG) for n in range(2)] for k, per in (("fetch_done", SUB), ("stashed", 1)))
    else:
        norm0 = Norm(ph, "norm0")
        lonely_added = S("lonely_added")
        x3 = ph.sb("x3", rows4)
        x3_stored = ph.dma_sems("x3_stored")
    pads_zero = ph.sem("pads_zero")
    h1_rows, h2_rows = (node_rows(tables[n], SLOTS) for n in (("h1", "h2") if sage else ("r1", "r2")))
    block = ph.block()

    def load_rows(eng, tile, arrived, g):
        if not sage:
            eng.dma_start(tile[:, g.b], at(node_rows(tables["x2"], SLOTS), g)).then_inc(arrived.of(g), 16)
        elif g.number == NG - 1:
            eng.dma_start(tile[0:NODE_TAIL, g.b], x[(NG - 1) * GROUP:N_NODES].rearrange("(p s) d -> p s d", s=SUB)).then_inc(arrived.of(g), 16)
        else:
            whole = x[0:(NG - 1) * GROUP].rearrange("(g p s) d -> g p s d", p=P, s=SUB)
            eng.dma_start(tile[:, g.b], at(whole, g)).then_inc(arrived.of(g), 16)

    @block.sync
    def _(sp):
        def load(g):
            if sage:
                wait_for(sp, turned, g.lag(2))
                if g.number == NG - 1:
                    sp.wait_ge(pads_zero, 1)
            else:
                wait_for(sp, norm0.done, g.lag(2))
            load_rows(sp, x_in, x_loaded, g)

        def reload(g):
            wait_for(sp, y_summed, g.lag(2))
            settle(ph, sp, g)
            if sage:
                if g.number == NG - 1:
                    sp.wait_ge(pads_zero, 2)
                load_rows(sp, x_again, x_reloaded, g)
            else:
                wait_for(sp, x3_stored, g)
                sp.dma_start(x_again[:, g.b], at(node_rows(tables["x3"], SLOTS), g)).then_inc(x_reloaded.of(g), 16)

        def store_x3(g):
            wait_for(sp, norm0.done, g)
            sp.dma_start(at(node_rows(tables["x3"], SLOTS), g), x3[:, g.b]).then_inc(x3_stored.of(g), 16)

        def store_h1(g):
            wait_for(sp, h1_out, g)
            sp.dma_start(at(h1_rows, g), h1[:, g.b]).then_inc(h1_stored.of(g), 16)

        def store_h2(g):
            wait_for(sp, h2_out, g)
            sp.dma_start(at(h2_rows, g), h2[:, g.b]).then_inc(h2_stored.of(g), 16)

        def store_y(g):
            if sage:
                wait_for(sp, norm2.done, g)
                sp.dma_start(at(node_rows(tables["x2"], SLOTS), g), x2[:, g.b]).then_inc(y_stored.of(g), 16)
                return
            wait_for(sp, norm.done, g)
            if g.number == NG - 1:
                sp.dma_start(out[(NG - 1) * GROUP:N_NODES].rearrange("(p s) d -> p s d", s=SUB), z[0:NODE_TAIL, g.b]).then_inc(y_stored.of(g), 16)
            else:
                whole = out[0:(NG - 1) * GROUP].rearrange("(g p s) d -> g p s d", p=P, s=SUB)
                sp.dma_start(at(whole, g), z[:, g.b]).then_inc(y_stored.of(g), 16)

        def store_u(g):
            wait_for(sp, u_out, g)
            sp.dma_start(at(node_rows(tables["u"], SLOTS), g), u[:, g.b, :, 0:D]).then_inc(u_stored.of(g), 16)
            wait_for(sp, att_out, g)
            sp.dma_start(at(node_rows(tables["att1"], SLOTS), g), att[:, g.b]).then_inc(att_stored.of(g), 16)
        if sage:
            stages = [(load, -1), (reload, 3), (store_h1, 3), (store_h2, 4), (store_u, 7), (store_y, 6)]
        else:
            stages = [(load, -1), (reload, 4), (store_x3, 2), (store_h1, 4), (store_h2, 5), (store_y, 6)]
        run_groups(sp, NG, stages)
        for stored in (h1_stored, h2_stored, y_stored) + ((u_stored, att_stored) if sage else (x3_stored,)):
            wait_for_all(sp, stored)

    @block.gpsimd
    def _(pool):
        if sage:
            def stash(g):
                for n in range(2):
                    pool_gather(pool, ph, g, (K.src_x, K.dst_x)[n], rings[n], ring_ready[n], stashed[n], x, fetched[n], fetch_done[n])

            def put(g):
                for n in range(2):
                    wait_for(pool, fetch_done[n], g)
                    settle(ph, pool, g)
                    pool.dma_start(at(slot_rows(tables[("x_msg", "x_own")[n]]), g), fetched[n][:, g.b]).then_inc(stashed[n].of(g), 16)
            run_groups(pool, EG, [(put, 1), (stash, 0)])
            for n in range(2):
                wait_for_all(pool, stashed[n])
            last = Group(0, NG - 1)
            wait_for(pool, turned, last.lag(2))
            pool.memset(x_in[:, last.b], 0.0).then_inc(pads_zero, 1)
            wait_for(pool, y_summed, last.lag(2))
            pool.memset(x_again[:, last.b], 0.0).then_inc(pads_zero, 1)

    @block.tensor
    def _(pe):
        def turn_x(g):
            if sage:
                wait_for(pe, x_loaded, g)
                wait_for(pe, x1_copied, g.lag(6))
            else:
                wait_for(pe, norm0.done, g)
            wait_for(pe, x_copied, g.lag(1))
            turn_rows(pe, bank_x, (x_in if sage else x3)[:, g.b], K.ident).then_inc(turned.sem, 1)

        def make_h1(g):
            wait_for(pe, x_copied, g)
            wait_for(pe, h1_kept, g.lag(1))
            layer_t(pe, h1_ps, [(w0, x_t[:, g.b])]).then_inc(h1_made.sem, 1)

        def make_h2(g):
            wait_for(pe, h1_kept, g)
            wait_for(pe, h2_kept, g.lag(1))
            layer_t(pe, h2_ps, [(w1, h1_t[:, g.b])]).then_inc(h2_made.sem, 1)

        def turn_h1(g):
            wait_for(pe, h1_out, g.lag(1))
            wait_for(pe, h2_out, g.lag(2))
            if sage:
                wait_for(pe, u_out, g.lag(4))
            turn_back(pe, ring, h1_t[:, g.b], range(SUB), K.ident).then_inc(h1_turned.sem, 1)

        def turn_h2(g):
            wait_for(pe, h2_kept, g)
            wait_for(pe, h1_out, g.lag(-1))
            wait_for(pe, h2_out, g.lag(1))
            if sage:
                wait_for(pe, u_out, g.lag(3))
            turn_back(pe, ring, h2_t[:, g.b], range(SUB), K.ident).then_inc(h2_turned.sem, 1)

        def make_y(g):
            wait_for(pe, h2_kept, g)
            wait_for(pe, y_biased, g.lag(1))
            layer_rows(pe, lanes(bank_y, D), [(w2, h2_t[:, g.b])]).then_inc(y_made.sem, 1)

        def turn_x1(g):
            wait_for(pe, norm.done, g)
            wait_for(pe, x_copied, g.lag(-5))
            wait_for(pe, x1_copied, g.lag(1))
            turn_rows(pe, bank_x, z[:, g.b], K.ident).then_inc(x1_turned.sem, 1)

        def make_u(g):
            wait_for(pe, x1_copied, g)
            wait_for(pe, h2_out, g.lag(-2))
            wait_for(pe, u_out, g.lag(1))
            layer_rows(pe, ring[:, :, 0:D + 2], [(W.wide["gat1"][:, :, 0:D + 2], x1_t[:, g.b])]).then_inc(u_made.sem, 1)
        stages = [(make_h1, L + 1), (turn_x, L)] + ([(make_u, 6)] if sage else [])
        stages += [(make_h2, L + 2), (turn_h1, L + 2), (make_y, L + 3), (turn_h2, L + 3)]
        if sage:
            stages.append((turn_x1, 5))
        run_groups(pe, NG, stages)

    @block.scalar
    def _(act):
        def copy_x(g):
            wait_for(act, turned, g)
            wait_for(act, h1_made, g.lag(2))
            act.copy(x_t[:, g.b, 0, :], bank_x[:]).then_inc(x_copied.sem, 1)

        def keep_h(made, kept, ps, tile, bias, also):
            def keep(g):
                wait_for(act, made, g)
                for user in also:
                    wait_for(act, user, g.lag(2))
                for c in range(2):
                    ins = act.activation(tile[:, g.b, c, :], ps[:, c, :], ACT.Relu, bias=bias[:, c:c + 1])
                ins.then_inc(kept.sem, 1)
            return keep
        keep_h1 = keep_h(h1_made, h1_kept, h1_ps, h1_t, b0, (h2_made, h1_turned))
        keep_h2 = keep_h(h2_made, h2_kept, h2_ps, h2_t, b1, (y_made, h2_turned))

        def out_h1(g):
            wait_for(act, h1_turned, g)
            wait_for(act, h1_stored, g.lag(2))
            for half in range(2):
                ins = act.copy(h1[:, g.b, 2 * half:2 * half + 2, :], ring[:, 2 * half:2 * half + 2, :])
            ins.then_inc(h1_out.sem, 1)

        def out_h2(g):
            wait_for(act, h2_turned, g)
            wait_for(act, h2_stored, g.lag(2))
            for half in range(2):
                ins = act.copy(h2[:, g.b, 2 * half:2 * half + 2, :], ring[:, 2 * half:2 * half + 2, :])
            ins.then_inc(h2_out.sem, 1)

        def copy_x1(g):
            wait_for(act, x1_turned, g)
            wait_for(act, u_made, g.lag(2))
            act.copy(x1_t[:, g.b, 0, :], bank_x[:]).then_inc(x1_copied.sem, 1)

        def out_u(g):
            wait_for(act, u_made, g)
            wait_for(act, u_stored, g.lag(2))
            wait_for(act, u_biased, g.lag(2))
            for half in range(2):
                ins = act.copy(u[:, g.b, 2 * half:2 * half + 2, :], ring[:, 2 * half:2 * half + 2, 0:D + 2])
            ins.then_inc(u_out.sem, 1)
        def root(norm_):
            return lambda g: norm_.scalar_root(act, g, W.eps)
        stages = [(keep_h1, L + 1), (copy_x, L)]
        stages += [(out_u, 6), (root(norm), 4), (root(norm2), 5)] if sage else [(root(norm0), 0), (root(norm), 5)]
        stages += [(keep_h2, L + 2), (out_h1, L + 2), (out_h2, L + 3)] + ([(copy_x1, 5)] if sage else [])
        run_groups(act, NG, stages)

    @block.vector
    def _(dve):
        def add_lonely(g):
            wait_for(dve, x_loaded, g)
            dve.tensor_tensor(x_in[:, g.b], x_in[:, g.b], to_subs(W.lonely_row), ALU.add).then_inc(lonely_added.sem, 1)
            wait_for(dve, lonely_added, g)
            norm0.vector_moments(dve, g, x_in)

        def apply0(g):
            wait_for(dve, turned, g.lag(2))
            wait_for(dve, x3_stored, g.lag(2))
            norm0.vector_apply(dve, g, x_in, x3)

        def residual(g):
            wait_for(dve, y_made, g)
            wait_for(dve, norm.done, g.lag(2))
            dve.tensor_tensor(y[:, g.b], lanes(bank_y, D), to_subs(b2), ALU.add).then_inc(y_biased.sem, 1)
            wait_for(dve, x_reloaded, g)
            wait_for(dve, y_biased, g)
            if sage:
                dve.scalar_tensor_tensor(y[:, g.b], y[:, g.b], 0.0, x_again[:, g.b], ALU.max, ALU.add).then_inc(y_summed.sem, 1)
            else:
                dve.tensor_tensor(y[:, g.b], y[:, g.b], x_again[:, g.b], ALU.add).then_inc(y_summed.sem, 1)
            wait_for(dve, y_summed, g)
            norm.vector_moments(dve, g, y)

        def apply(g):
            if sage:
                wait_for(dve, x1_turned, g.lag(2))
            else:
                wait_for(dve, y_stored, g.lag(2))
            norm.vector_apply(dve, g, y, z)

        def second(g):
            wait_for(dve, norm.done, g)
            wait_for(dve, y_stored, g.lag(2))
            dve.scalar_tensor_tensor(x2[:, g.b], z[:, g.b], 0.0, z[:, g.b], ALU.max, ALU.add).then_inc(z_summed.sem, 1)
            wait_for(dve, z_summed, g)
            norm2.vector_moments(dve, g, x2)

        def apply2(g):
            norm2.vector_apply(dve, g, x2, x2)

        def count_u(g):
            wait_for(dve, u_out, g)
            wait_for(dve, att_stored, g.lag(2))
            dve.tensor_copy(att[:, g.b], u[:, g.b, :, D:D + 2]).then_inc(att_out.sem, 1)
            dve.tensor_tensor(ub[:, g.b], u[:, g.b, :, 0:D], to_subs(W.row["gat1_b"]), ALU.add).then_inc(u_biased.sem, 1)
            wait_for(dve, u_biased, g)
            settle(ph, dve, g)
            for s in range(SUB):
                ins = dve.bn_stats(tables["node_stats"][:, cols(g, SUB, s, 1), :], ub[:, g.b, s, :])
            ins.then_inc(u_counted.sem, 1)
        if sage:
            stages = [(residual, 4), (apply, 5), (second, 5), (apply2, 6), (count_u, 6)]
        else:
            stages = [(apply0, 1), (residual, 5), (add_lonely, 0), (apply, 6)]
        run_groups(dve, NG, stages)
    ph.close()



class SegmentSums:

    def __init__(self, ph, K, table, index, width, weights, own=None, own_weights=None):
        self.ph, self.K, self.table, self.index = ph, K, table, index
        self.chunks, self.weights, self.own_view, self.own_weights = width // P, weights, own, own_weights
        heads = len(weights)
        assert heads == 1 or self.chunks == 1
        self.msg = ph.sb("msg", [P, 2, SUB, width])
        if index is None:
            self.arrived = ph.dma_sems("arrived")
        else:
            self.ring = ph.sb("ring", [P, 2, SUB], I32)
            self.ring_ready, self.arrived = ph.count_sem("ring_ready"), ph.dma_sems("arrived", SUB)
        self.weighted = ph.sb("weighted", [P, 2, heads, GROUP])
        self.sum_t = ph.sb("sum_t", [P, 2, self.chunks, GROUP])
        self.ps = [ph.ps(f"sum_ps{b}", [P, self.chunks, GROUP]) for b in range(2)]
        self.is_weighted, self.summed, self.carried = ph.count_sem("is_weighted"), ph.count_sem("summed", SUB), ph.count_sem("carried", SUB * self.chunks)
        self.zeroed = ph.sem("zeroed")
        self.rows, self.messages, self.used = self.msg, self.arrived, self.summed
        if own is not None:
            self.own, self.own_in = ph.sb("own", [P, 2, SUB, width]), ph.dma_sems("own_in")
            self.diag, self.diag_made = ph.sb("diag", [P, 2, heads, GROUP]), ph.count_sem("diag_made")

    def pool_fetch(self, pool, g):
        pool_gather(pool, self.ph, g, self.index, self.ring, self.ring_ready, self.used, self.table, self.msg, self.arrived)

    def sync_messages(self, sp, g):
        wait_for(sp, self.summed, g.lag(2))
        sp.dma_start(self.msg[:, g.b], at(slot_rows(self.table), g)).then_inc(self.arrived.of(g), 16)

    def sync_own(self, sp, g):
        wait_for(sp, self.summed, g.lag(2))
        sp.dma_start(self.own[:, g.b], at(self.own_view, g)).then_inc(self.own_in.of(g), 16)

    def scalar_weigh(self, act, g):
        wait_for(act, self.summed, g.lag(2))
        settle(self.ph, act, g)
        for h, weight in enumerate(self.weights):
            for s in range(SUB):
                if self.own_view is not None and h == 0:
                    act.activation(self.diag[:, g.b, h, s * P:(s + 1) * P], self.K.ident[:], ACT.Copy,
                                   scale=self.own_weights[h][:, cols(g, SUB, s, 1)])
                ins = act.activation(self.weighted[:, g.b, h, s * P:(s + 1) * P], self.K.same[:, cols(g, GROUP, s * P, P)],
                                     ACT.Copy, scale=weight[:, cols(g, SUB, s, 1)])
        ins.then_inc(self.is_weighted.sem, 1)

    def vector_diag(self, dve, g):
        wait_for(dve, self.summed, g.lag(2))
        for s in range(SUB):
            ins = dve.tensor_scalar(self.diag[:, g.b, 1, s * P:(s + 1) * P], self.K.ident[:],
                                    self.own_weights[1][:, cols(g, SUB, s, 1)], None, ALU.mult)
        ins.then_inc(self.diag_made.sem, 1)

    def tensor_sum(self, pe, g):
        wait_for(pe, self.messages, g)
        wait_for(pe, self.is_weighted, g)
        if self.own_view is not None:
            wait_for(pe, self.own_in, g)
            if len(self.weights) == 2:
                wait_for(pe, self.diag_made, g)
        wait_for(pe, self.carried, g.lag(2))
        heads, ps = len(self.weights), self.ps[g.b]
        for s in range(SUB):
            at_s = slice(s * P, (s + 1) * P)
            for c in range(self.chunks):
                for h in range(heads):
                    m = P // heads
                    f = slice(c * P + h * m, c * P + (h + 1) * m)
                    out = ps[h * m:(h + 1) * m, c, at_s]
                    mm = pe.matmul(out, self.rows[:, g.b, s, f], self.weighted[:, g.b, h, at_s], start=True, stop=self.own_view is None)
                    if self.own_view is not None:
                        mm = pe.matmul(out, self.own[:, g.b, s, f], self.diag[:, g.b, h, at_s], start=False, stop=True)
            mm.then_inc(self.summed.sem, 1)

    def vector_zero(self, dve):
        dve.memset(self.sum_t[:, 1, :, GROUP - 1:GROUP], 0.0).then_inc(self.zeroed, 1)
        dve.wait_ge(self.zeroed, 1)

    def vector_carry(self, dve, g, used):
        wait_for(dve, self.summed, g)
        for user in used:
            wait_for(dve, user, g.lag(2))
        for s in range(SUB):
            if s == 0:
                wait_for(dve, self.carried, g.lag(1))
            else:
                wait_for(dve, self.carried, g, s * self.chunks)
            for c in range(self.chunks):
                now = self.sum_t[:, g.b, c, :]
                before = now[:, s * P - 1:s * P] if s else self.sum_t[:, 1 - g.b, c, GROUP - 1:GROUP]
                dve.scalar_tensor_tensor(now[:, s * P:(s + 1) * P], self.K.goes_on[:, cols(g, GROUP, s * P, P)], before,
                                         self.ps[g.b][:, c, s * P:(s + 1) * P], ALU.mult, ALU.add).then_inc(self.carried.sem, 1)


def slot_hidden_block(nc, name, K, W, tables, src_meta=None):
    sage, first = name.startswith("sage"), name.endswith("0")
    ph = Phase(nc, name, EG)
    S, A_ = ph.count_sem, ph.dma_sems
    if sage:
        table, index, width = (tables["x_msg"], None, D) if first else (tables["h1"], K.idx, HID)
        sums = SegmentSums(ph, K, table, index, width, [K.inv_deg])
        w_own, w_sum = (W.m[n] for n in (("ws0", "wn0") if first else ("ws1", "wn1")))
        bias, out_rows, out_t = (W.col["b0_c"], "h1", "h1_t") if first else (W.col["b1_c"], "h2", "h2_t")
        own_t = ph.sb("own_t", [P, 2, width // P, GROUP])
        own_ready = S("own_ready") if first else A_("own_ready")
        if first:
            own, own_arrived, own_turned = ph.sb("own_rows", [P, 2, SUB, D]), A_("own_arrived"), S("own_turned")
            small = SmallGather(ph, tables["meta"], 2, K.src_node, src_meta)
            own_ps = ph.ps("own_ps", [P, GROUP])
    else:
        table, width = tables["x3" if first else "r1"], D if first else HID
        sums = SegmentSums(ph, K, table, K.idx, width, [K.dinv], own=slot_rows(table), own_weights=[K.dinv_last])
        w_sum, bias, out_rows = (W.m["gcn0"], W.col["gcn0_b_c"], "r1") if first else (W.m["gcn1"], W.col["gcn1_b_c"], "r2")
    h_t, h = ph.sb("h_t", [P, 2, 2, GROUP]), ph.sb("h", [P, 2, SUB, HID])
    h_ps = ph.ps("h_ps", [P, 2, GROUP])
    turn_ps = [ph.ps(f"turn{k}", [P, 2, HID]) for k in range(2)]
    made, kept, turned, out_a, out_b = (S(n) for n in ("made", "kept", "turned", "out_a", "out_b"))
    h_stored, ht_stored = A_("h_stored"), A_("ht_stored")
    block = ph.block()

    @block.sync
    def _(sp):
        def load_own(g):
            if not sage:
                sums.sync_own(sp, g)
            elif first:
                wait_for(sp, own_turned, g.lag(2))
                sp.dma_start(own[:, g.b], at(slot_rows(tables["x_own"]), g)).then_inc(own_arrived.of(g), 16)
            else:
                wait_for(sp, made, g.lag(2))
                sp.dma_start(own_t[:, g.b], at(tables["h1_t"], g)).then_inc(own_ready.of(g), 16)

        def store_t(g):
            wait_for(sp, kept, g)
            sp.dma_start(at(tables[out_t], g), h_t[:, g.b]).then_inc(ht_stored.of(g), 16)

        def store(g):
            wait_for(sp, out_a, g)
            wait_for(sp, out_b, g)
            sp.dma_start(at(slot_rows(tables[out_rows]), g), h[:, g.b]).then_inc(h_stored.of(g), 16)
        stages = [(load_own, 0 if sage and not first else -1), (store, 3)]
        if sage:
            stages.append((store_t, 2))
        if sage and first:
            stages.insert(0, (lambda g: sums.sync_messages(sp, g), -1))
        run_groups(sp, EG, stages)
        wait_for_all(sp, h_stored)
        if sage:
            wait_for_all(sp, ht_stored)

    @block.gpsimd
    def _(pool):
        fetch = small.pool_fetch if sage and first else sums.pool_fetch
        run_groups(pool, EG, [(lambda g: fetch(pool, g), 0)])

    @block.tensor
    def _(pe):
        def turn_own(g):
            wait_for(pe, own_arrived, g)
            wait_for(pe, own_ready, g.lag(1))
            turn_rows(pe, own_ps, own[:, g.b], K.ident).then_inc(own_turned.sem, 1)

        def make(g):
            wait_for(pe, sums.carried, g)
            wait_for(pe, kept, g.lag(1))
            parts = [(w_sum, sums.sum_t[:, g.b])]
            if sage:
                wait_for(pe, own_ready, g)
                parts.append((w_own, own_t[:, g.b]))
            layer_t(pe, h_ps, parts).then_inc(made.sem, 1)

        def turn(g):
            wait_for(pe, kept, g)
            wait_for(pe, out_a, g.lag(1))
            wait_for(pe, out_b, g.lag(1))
            turn_back(pe, turn_ps[0], h_t[:, g.b], (0, 1), K.ident)
            turn_back(pe, turn_ps[1], h_t[:, g.b], (2, 3), K.ident).then_inc(turned.sem, 1)
        stages = [(lambda g: sums.tensor_sum(pe, g), 0), (make, 1), (turn, 2)]
        if sage and first:
            stages.insert(1, (turn_own, 0))
        run_groups(pe, EG, stages)

    @block.scalar
    def _(act):
        def copy_own(g):
            wait_for(act, own_turned, g)
            wait_for(act, made, g.lag(2))
            act.copy(own_t[:, g.b, 0, :], own_ps[:]).then_inc(own_ready.sem, 1)

        def keep(g):
            wait_for(act, made, g)
            wait_for(act, turned, g.lag(2))
            if sage:
                wait_for(act, ht_stored, g.lag(2))
            for c in range(2):
                ins = act.activation(h_t[:, g.b, c, :], h_ps[:, c, :], ACT.Relu, bias=bias[:, c:c + 1])
            ins.then_inc(kept.sem, 1)

        def out(g):
            wait_for(act, turned, g)
            wait_for(act, h_stored, g.lag(2))
            if sage:
                act.copy(h[:, g.b, 0:2, :], turn_ps[0][:]).then_inc(out_a.sem, 1)
                return
            settle(ph, act, g)
            for s in range(2):
                ins = act.activation(h[:, g.b, s, :], turn_ps[0][:, s, :], ACT.Copy, scale=K.dinv[:, cols(g, SUB, s, 1)])
            ins.then_inc(out_a.sem, 1)
        stages = [(lambda g: sums.scalar_weigh(act, g), -1), (keep, 1), (out, 2)]
        if sage and first:
            stages.insert(1, (copy_own, 0))
        run_groups(act, EG, stages)

    @block.vector
    def _(dve):
        sums.vector_zero(dve)

        def out(g):
            wait_for(dve, turned, g)
            wait_for(dve, h_stored, g.lag(2))
            if sage:
                dve.tensor_copy(h[:, g.b, 2:4, :], turn_ps[1][:]).then_inc(out_b.sem, 1)
                return
            for s in range(2):
                ins = dve.tensor_scalar(h[:, g.b, 2 + s, :], turn_ps[1][:, s, :], K.dinv[:, cols(g, SUB, 2 + s, 1)], None, ALU.mult)
            ins.then_inc(out_b.sem, 1)
        stages = [(lambda g: sums.vector_carry(dve, g, [made]), 0), (out, 2)]
        if sage and first:
            stages.append((lambda g: small.vector_keep(dve, g), 0))
        run_groups(dve, EG, stages)
    ph.close()


def slot_out_block(nc, name, K, W, tables, out_dram):
    sage = name == "sage"
    ph = Phase(nc, f"{name}_end", EG)
    S, A_ = ph.count_sem, ph.dma_sems
    rows4 = [P, 2, SUB, D]
    if sage:
        sums = SegmentSums(ph, K, tables["h2"], K.idx, HID, [K.inv_deg])
        own_t, own_ready = ph.sb("own_t", [P, 2, 2, GROUP]), A_("own_ready")
        before, bias = tables["x_own"], W.row["b2"]
        x1_t, u = ph.sb("x1_t", [P, 2, 1, GROUP]), ph.sb("u", [P, 2, SUB, D + 4])
        x1_ps, u_ps = ph.ps("x1_ps", [P, GROUP]), ph.ps("u_ps", [P, SUB, HID])
        x1_turned, x1_copied, u_made, u_out, att_out = (S(n) for n in ("x1_turned", "x1_copied", "u_made", "u_out", "att_out"))
        u_stored, att_stored = A_("u_stored"), A_("att_stored")
    else:
        sums = SegmentSums(ph, K, tables["r2"], K.idx, HID, [K.dinv], own=slot_rows(tables["r2"]), own_weights=[K.dinv_last])
        before, bias = tables["x3_own"], W.row["gcn2_b"]
        to_ring, to_ring_ready = ph.sb("to_ring", [P, 2, SUB], I32), S("to_ring_ready")
        scattered = A_("scattered", SUB)
    x_in, y, z = (ph.sb(n, rows4) for n in ("x_in", "y", "z"))
    y_ps = ph.ps("y_ps", [P, GROUP])
    norm = Norm(ph, "norm")
    x_loaded, z_stored = A_("x_loaded"), A_("z_stored")
    made, biased, added = S("made"), S("biased"), S("added")
    block = ph.block()

    @block.sync
    def _(sp):
        def load_own(g):
            if sage:
                wait_for(sp, made, g.lag(2))
                sp.dma_start(own_t[:, g.b], at(tables["h2_t"], g)).then_inc(own_ready.of(g), 16)
            else:
                sums.sync_own(sp, g)

        def load_x(g):
            wait_for(sp, added, g.lag(2))
            sp.dma_start(x_in[:, g.b], at(slot_rows(before), g)).then_inc(x_loaded.of(g), 16)

        def store_x1(g):
            wait_for(sp, norm.done, g)
            sp.dma_start(at(slot_rows(tables["x1"]), g), z[:, g.b]).then_inc(z_stored.of(g), 16)

        def store_u(g):
            wait_for(sp, u_out, g)
            sp.dma_start(at(slot_rows(tables["u"]), g), u[:, g.b, :, 0:D]).then_inc(u_stored.of(g), 16)
            wait_for(sp, att_out, g)
            with nc.allow_non_contiguous_dma(reason="two heads' scores to a row"):
                sp.dma_start(at(slot_rows(tables["att1"]), g), K.att[:, cols(g, SUB), 0:2]).then_inc(att_stored.of(g), 16)
        stages = [(load_own, 0 if sage else -1), (load_x, 0)] + ([(store_x1, 3), (store_u, 4)] if sage else [])
        run_groups(sp, EG, stages)
        if sage:
            for stored in (z_stored, u_stored, att_stored):
                wait_for_all(sp, stored)

    @block.gpsimd
    def _(pool):
        def scatter(g):
            wait_for(pool, norm.done, g)
            wait_for(pool, scattered, g.lag(2))
            settle(ph, pool, g)
            pool.tensor_copy(to_ring[:, g.b, :], K.idx_out[:, cols(g, SUB)]).then_inc(to_ring_ready.sem, 1)
            wait_for(pool, to_ring_ready, g)
            settle(ph, pool, g)
            for s in range(SUB):
                pool.indirect_dma_start(out=out_dram, out_offset=bass.IndirectOffsetOnAxis(ap=to_ring[:, g.b, s:s + 1], axis=0),
                                        in_=z[:, g.b, s, :], in_offset=None, bounds_check=N_NODES - 1, oob_is_err=False).then_inc(scattered.of(g), 16)
        stages = [(lambda g: sums.pool_fetch(pool, g), 0)] + ([] if sage else [(scatter, 4)])
        run_groups(pool, EG, stages)
        if not sage:
            wait_for_all(pool, scattered)

    @block.tensor
    def _(pe):
        def make(g):
            wait_for(pe, sums.carried, g)
            wait_for(pe, biased, g.lag(1))
            parts = [(W.m["wn2" if sage else "gcn2"], sums.sum_t[:, g.b])]
            if sage:
                wait_for(pe, own_ready, g)
                parts.append((W.m["ws2"], own_t[:, g.b]))
            layer_rows(pe, lanes(y_ps, D), parts).then_inc(made.sem, 1)

        def turn_x1(g):
            wait_for(pe, norm.done, g)
            wait_for(pe, x1_copied, g.lag(1))
            turn_rows(pe, x1_ps, z[:, g.b], K.ident).then_inc(x1_turned.sem, 1)

        def make_u(g):
            wait_for(pe, x1_copied, g)
            wait_for(pe, u_out, g.lag(1))
            layer_rows(pe, u_ps[:, :, 0:D + 4], [(W.wide["gat1"], x1_t[:, g.b])]).then_inc(u_made.sem, 1)
        stages = [(lambda g: sums.tensor_sum(pe, g), 0)] + ([(make_u, 3), (make, 1), (turn_x1, 2)] if sage else [(make, 1)])
        run_groups(pe, EG, stages)

    @block.scalar
    def _(act):
        def copy_x1(g):
            wait_for(act, x1_turned, g)
            wait_for(act, u_made, g.lag(2))
            act.copy(x1_t[:, g.b, 0, :], x1_ps[:]).then_inc(x1_copied.sem, 1)

        def out_u(g):
            wait_for(act, u_made, g)
            wait_for(act, u_stored, g.lag(2))
            wait_for(act, att_out, g.lag(2))
            for half in range(2):
                ins = act.copy(u[:, g.b, 2 * half:2 * half + 2, :], u_ps[:, 2 * half:2 * half + 2, 0:D + 4])
            ins.then_inc(u_out.sem, 1)
        weigh = (lambda g: sums.scalar_weigh(act, g), -2)
        stages = [(out_u, 3), weigh, (copy_x1, 2)] if sage else [weigh]
        stages.append((lambda g: norm.scalar_root(act, g, W.eps), 1))
        run_groups(act, EG, stages)

    @block.vector
    def _(dve):
        sums.vector_zero(dve)

        def add(g):
            wait_for(dve, made, g)
            wait_for(dve, norm.done, g.lag(2))
            dve.tensor_tensor(y[:, g.b], lanes(y_ps, D), to_subs(bias), ALU.add).then_inc(biased.sem, 1)
            wait_for(dve, x_loaded, g)
            wait_for(dve, biased, g)
            if sage:
                dve.scalar_tensor_tensor(y[:, g.b], y[:, g.b], 0.0, x_in[:, g.b], ALU.max, ALU.add).then_inc(added.sem, 1)
            else:
                dve.tensor_tensor(y[:, g.b], y[:, g.b], x_in[:, g.b], ALU.add).then_inc(added.sem, 1)
            wait_for(dve, added, g)
            norm.vector_moments(dve, g, y)

        def apply(g):
            if sage:
                wait_for(dve, x1_turned, g.lag(2))
                wait_for(dve, z_stored, g.lag(2))
            else:
                wait_for(dve, scattered, g.lag(2))
            norm.vector_apply(dve, g, y, z)

        def out_att(g):
            wait_for(dve, u_out, g)
            settle(ph, dve, g)
            dve.tensor_copy(K.att[:, cols(g, SUB), :], u[:, g.b, :, D:D + 4]).then_inc(att_out.sem, 1)
        stages = [(lambda g: sums.vector_carry(dve, g, [made]), 0)] + ([(out_att, 3)] if sage else []) + [(apply, 2), (add, 1)]
        run_groups(dve, EG, stages)
    ph.close()



def softmax_block(nc, name, K, source_scores, heads):
    ph = Phase(nc, name, 0)
    R = [RQ, RJ]
    a_src, a_dst, a_own, e_self, top, share, total = (ph.sb(n, R) for n in ("a_src", "a_dst", "a_own", "e_self", "top", "share", "total"))
    into_ps = [ph.ps(f"into{b}", [P, RJ]) for b in range(2)]
    outof_ps = [ph.ps(f"outof{b}", [P, RQ]) for b in range(2)]
    chain, turned, turn_read, ready, outof, outof_read, to_exp, from_exp = (
        ph.sem(n) for n in ("chain", "turned", "turn_read", "ready", "outof", "outof_read", "to_exp", "from_exp"))
    per_head = 5
    seg = Segments(ph, K, heads * per_head)
    block = ph.block()

    @block.tensor
    def _(pe):
        n = m = 0
        for h in range(heads):
            for tile in (source_scores[:, :, h], K.att[:, :, heads + h], K.att[:, :, h]):
                if n >= 2:
                    pe.wait_ge(turn_read, n - 1)
                for half in range(2):
                    mm = pe.transpose(into_ps[n % 2][0:RQ, half * P:(half + 1) * P], tile[:, half::2], K.ident[:])
                mm.then_inc(turned, 1)
                n += 1
            seg.tensor_side(pe, h * per_head, (h + 1) * per_head)
            pe.wait_ge(ready, h + 1)
            for tile in (share, e_self):
                for half in range(2):
                    if m >= 2:
                        pe.wait_ge(outof_read, m - 1)
                    pe.transpose(outof_ps[m % 2][:], tile[:, half * P:(half + 1) * P], K.ident[0:RQ, 0:RQ]).then_inc(outof, 1)
                    m += 1

    @block.scalar
    def _(act):
        for h in range(heads):
            act.wait_ge(to_exp, h + 1)
            act.activation(share[:], share[:], ACT.Exp)
            act.activation(e_self[:], e_self[:], ACT.Exp).then_inc(from_exp, 1)

    @block.vector
    def _(dve):
        link = linker(dve, chain)
        n = m = 0
        for h in range(heads):
            for tile in (a_src, a_dst, a_own):
                dve.wait_ge(turned, n + 1)
                dve.tensor_copy(tile[:], into_ps[n % 2][0:RQ, :]).then_inc(turn_read, 1)
                n += 1
            dve.wait_ge(turn_read, n)
            link(dve.tensor_tensor(e_self[:], a_own[:], a_dst[:], ALU.add))
            link(dve.scalar_tensor_tensor(e_self[:], e_self[:], 0.2, e_self[:], ALU.mult, ALU.max))
            seg.spread_last(dve, link, a_dst[:], a_dst[:])
            link(dve.tensor_tensor(share[:], a_src[:], a_dst[:], ALU.add))
            link(dve.scalar_tensor_tensor(share[:], share[:], 0.2, share[:], ALU.mult, ALU.max))
            seg.running_max(dve, link, top[:], share[:])
            link(dve.tensor_tensor(top[:], top[:], e_self[:], ALU.max))
            seg.spread_last(dve, link, top[:], top[:])
            dve.tensor_tensor(share[:], share[:], top[:], ALU.subtract)
            link(dve.tensor_tensor(e_self[:], e_self[:], top[:], ALU.subtract))
            link(dve.tensor_tensor(share[:], share[:], K.real[:], ALU.mult))
            dve.tensor_tensor(e_self[:], e_self[:], K.last[:], ALU.mult).then_inc(to_exp, 1)
            dve.wait_ge(from_exp, h + 1)
            seg.running_sum(dve, link, total[:], share[:])
            link(dve.tensor_tensor(total[:], total[:], e_self[:], ALU.add))
            seg.spread_last(dve, link, total[:], total[:])
            link(dve.tensor_scalar(total[:], total[:], 1e-16, None, ALU.add))
            link(dve.reciprocal(total[:], total[:]))
            dve.tensor_tensor(total[:], total[:], K.real[:], ALU.mult)
            link(dve.tensor_tensor(e_self[:], e_self[:], K.last[:], ALU.mult))
            link(dve.tensor_tensor(share[:], share[:], total[:], ALU.mult))
            dve.tensor_tensor(e_self[:], e_self[:], total[:], ALU.mult).then_inc(ready, 1)
            for result in (K.alpha, K.alpha_self):
                for half in range(2):
                    dve.wait_ge(outof, m + 1)
                    dve.tensor_copy(result[:, h, half::2], outof_ps[m % 2][:]).then_inc(outof_read, 1)
                    m += 1
            dve.wait_ge(outof_read, m)
    ph.close()


def attend_block(nc, name, K, W, tables):
    first = name == "gat1"
    ph = Phase(nc, name, EG)
    S, A_ = ph.count_sem, ph.dma_sems
    table, index = (tables["u"] if first else tables["yv"][0:V_ROWS], K.idx)
    heads = range(2 if first else 1)
    sums = SegmentSums(ph, K, table, index, D, [K.alpha[:, h, :] for h in heads],
                       own=slot_rows(table), own_weights=[K.alpha_self[:, h, :] for h in heads])
    bias = W.row["gat1_b" if first else "gat2_b"]
    g_ps = [ph.ps(f"g_ps{b}", [P, GROUP]) for b in range(2)]
    rows, biased = ph.sb("rows", [P, 2, SUB, D]), ph.sb("biased", [P, 2, SUB, D])
    turned, out_done, is_biased, counted = S("turned"), S("out_done"), S("is_biased"), S("counted")
    stored = A_("stored")
    block = ph.block()

    @block.sync
    def _(sp):
        def store(g):
            if first:
                wait_for(sp, sums.carried, g)
                sp.dma_start(at(tables["g_t"], g), sums.sum_t[:, g.b]).then_inc(stored.of(g), 16)
            else:
                wait_for(sp, out_done, g)
                settle(ph, sp, g)
                sp.dma_start(at(slot_rows(tables["yv"], V_ROWS), g), rows[:, g.b]).then_inc(stored.of(g), 16)
        run_groups(sp, EG, [(lambda g: sums.sync_own(sp, g), -1), (store, 1 if first else 2)])
        wait_for_all(sp, stored)

    @block.gpsimd
    def _(pool):
        run_groups(pool, EG, [(lambda g: sums.pool_fetch(pool, g), 0)])

    @block.tensor
    def _(pe):
        def turn(g):
            wait_for(pe, sums.carried, g)
            wait_for(pe, out_done, g.lag(2))
            turn_back(pe, lanes(g_ps[g.b], D), sums.sum_t[:, g.b], range(SUB), K.ident).then_inc(turned.sem, 1)
        run_groups(pe, EG, [(lambda g: sums.tensor_sum(pe, g), 0), (turn, 1)])

    @block.scalar
    def _(act):
        def out(g):
            wait_for(act, turned, g)
            wait_for(act, is_biased, g.lag(2))
            if not first:
                wait_for(act, stored, g.lag(2))
            act.copy(rows[:, g.b], lanes(g_ps[g.b], D)).then_inc(out_done.sem, 1)
        run_groups(act, EG, [(lambda g: sums.scalar_weigh(act, g), -1), (out, 1)])

    @block.vector
    def _(dve):
        sums.vector_zero(dve)

        def carry(g):
            if first:
                wait_for(dve, stored, g.lag(2))
            sums.vector_carry(dve, g, [turned])

        def count(g):
            wait_for(dve, out_done, g)
            dve.tensor_tensor(biased[:, g.b], rows[:, g.b], to_subs(bias), ALU.add).then_inc(is_biased.sem, 1)
            wait_for(dve, is_biased, g)
            settle(ph, dve, g)
            for s in range(SUB):
                ins = dve.bn_stats(tables["slot_stats"][:, cols(g, SUB, s, 1), :], biased[:, g.b, s, :])
            ins.then_inc(counted.sem, 1)
        run_groups(dve, EG, [(carry, 0), (count, 1)] + ([(lambda g: sums.vector_diag(dve, g), -2)] if first else []))
    ph.close()


def graph_norm_block(nc, name, K, W, tables):
    first = name == "ln1"
    ph = Phase(nc, name, 0)
    work, part = ph.sb("work", [P, NG * SUB]), ph.sb("part", [P, NG * SUB])
    sums, total, small = ph.sb("sums", [P, 4]), ph.sb("total", [P, 2]), ph.sb("small", [P, 4])
    sum_ps = ph.ps("sum_ps", [P, 4])
    chain, partial, summed, to_root, rooted = (ph.sem(n) for n in ("chain", "partial", "summed", "to_root", "rooted"))
    block = ph.block()

    @block.tensor
    def _(pe):
        pe.wait_ge(partial, 1)
        pe.matmul(sum_ps[:], K.ones[:], sums[:], start=True, stop=True).then_inc(summed, 1)

    @block.scalar
    def _(act):
        act.wait_ge(to_root, 1)
        act.activation(small[:, 2:3], small[:, 1:2], ACT.Sqrt, bias=W.eps[:]).then_inc(rooted, 1)

    @block.vector
    def _(dve):
        link = linker(dve, chain)
        node_mask = K.node_mask[:].rearrange("p g s -> p (g s)")
        for k, (stats, mask, n) in enumerate(((tables["node_stats"], node_mask, NG * SUB), (tables["slot_stats"], K.last_c[:], ET))):
            even, odd = stats[:, :, 1], stats[:, :, 4]
            w, q = work[:, 0:n], part[:, 0:n]
            link(dve.tensor_tensor(w, even, odd, ALU.add))
            link(dve.tensor_tensor(w, w, mask, ALU.mult))
            link(dve.tensor_reduce(sums[:, 2 * k:2 * k + 1], w, AX.X, ALU.add))
            link(dve.tensor_tensor(w, even, even, ALU.mult))
            link(dve.tensor_tensor(q, odd, odd, ALU.mult))
            link(dve.tensor_tensor(w, w, q, ALU.add))
            link(dve.tensor_tensor(q, stats[:, :, 2], stats[:, :, 5], ALU.add))
            link(dve.scalar_tensor_tensor(w, w, float(D // 2), q, ALU.mult, ALU.add))
            link(dve.tensor_tensor(w, w, mask, ALU.mult))
            link(dve.tensor_reduce(sums[:, 2 * k + 1:2 * k + 2], w, AX.X, ALU.add))
        dve.sem_inc(partial, 1)
        dve.wait_ge(summed, 1)
        link(dve.tensor_copy(small[:], sum_ps[:]))
        link(dve.tensor_tensor(total[:], small[:, 0:2], small[:, 2:4], ALU.add))
        count = float(N_NODES * D)
        mean, var, scale = small[:, 0:1], small[:, 1:2], small[:, 2:3]
        link(dve.tensor_scalar(mean, total[:, 0:1], D / 2 / count, None, ALU.mult))
        link(dve.tensor_tensor(small[:, 3:4], mean, mean, ALU.mult))
        link(dve.tensor_scalar(total[:, 1:2], total[:, 1:2], 1.0 / count, None, ALU.mult))
        link(dve.tensor_tensor(var, total[:, 1:2], small[:, 3:4], ALU.subtract))
        dve.sem_inc(to_root, 1)
        dve.wait_ge(rooted, 1)
        link(dve.reciprocal(scale, scale))
        scale_, shift = (W.ln1_scale, W.ln1_shift) if first else (W.ln2_scale, W.ln2_shift)
        bias, w, b = (W.col[n] for n in (("gat1_b_c", "ln1_w_c", "ln1_b_c") if first else ("gat2_b_c", "ln2_w_c", "ln2_b_c")))
        link(dve.tensor_tensor(scale_[:], w[:], scale, ALU.mult))
        link(dve.tensor_tensor(shift[:], bias[:], mean, ALU.subtract))
        link(dve.tensor_tensor(shift[:], shift[:], scale_[:], ALU.mult))
        link(dve.tensor_tensor(shift[:], shift[:], b[:], ALU.add))
    ph.close()


def second_product_block(nc, name, K, W, tables):
    nodes = name == "node_v"
    n = NG if nodes else EG
    ph = Phase(nc, name, n)
    S, A_ = ph.count_sem, ph.dma_sems
    rows4 = [P, 2, SUB, D]
    x_in = ph.sb("x_in", rows4 if nodes else [P, 2, 1, GROUP])
    x_t, v, biased, att = ph.sb("x_t", [P, 2, 1, GROUP]), ph.sb("v", [P, 2, SUB, D + 2]), ph.sb("biased", rows4), ph.sb("att", [P, 2, SUB, 2])
    x_ps, v_ps = ([ph.ps(f"{k}{b}", shape) for b in range(2)] for k, shape in (("x_ps", [P, GROUP]), ("v_ps", [P, SUB, HID])))
    loaded, v_stored, att_stored = A_("loaded"), A_("v_stored"), A_("att_stored")
    turned, normed, made, v_out, att_out, is_biased, counted = (S(k) for k in ("turned", "normed", "made", "v_out", "att_out", "is_biased", "counted"))
    source = node_rows(tables["u"], SLOTS) if nodes else tables["g_t"]
    v_rows = node_rows(tables["yv"], SLOTS) if nodes else slot_rows(tables["yv"])
    att_rows = node_rows(tables["att2"], SLOTS) if nodes else slot_rows(tables["att2"])
    block = ph.block()

    @block.sync
    def _(sp):
        def load(g):
            wait_for(sp, turned if nodes else normed, g.lag(2))
            sp.dma_start(x_in[:, g.b], at(source, g)).then_inc(loaded.of(g), 16)

        def store(g):
            wait_for(sp, v_out, g)
            sp.dma_start(at(v_rows, g), v[:, g.b, :, 0:D]).then_inc(v_stored.of(g), 16)
            wait_for(sp, att_out, g)
            sp.dma_start(at(att_rows, g), att[:, g.b]).then_inc(att_stored.of(g), 16)
        run_groups(sp, n, [(load, -1), (store, 2)])
        wait_for_all(sp, v_stored)
        wait_for_all(sp, att_stored)

    @block.tensor
    def _(pe):
        def turn(g):
            wait_for(pe, loaded, g)
            wait_for(pe, normed, g.lag(2))
            turn_rows(pe, x_ps[g.b], x_in[:, g.b], K.ident).then_inc(turned.sem, 1)

        def make(g):
            wait_for(pe, normed, g)
            wait_for(pe, v_out, g.lag(2))
            layer_rows(pe, v_ps[g.b][:, :, 0:D + 2], [(W.wide["gat2"], x_t[:, g.b])]).then_inc(made.sem, 1)
        run_groups(pe, n, ([(turn, 0)] if nodes else []) + [(make, 1)])

    @block.scalar
    def _(act):
        def norm(g):
            wait_for(act, turned if nodes else loaded, g)
            wait_for(act, made, g.lag(2))
            act.activation(x_t[:, g.b, 0, :], x_ps[g.b][:] if nodes else x_in[:, g.b, 0, :], ACT.Relu,
                           bias=W.ln1_shift[:], scale=W.ln1_scale[:]).then_inc(normed.sem, 1)

        def out(g):
            wait_for(act, made, g)
            wait_for(act, v_stored, g.lag(2))
            if nodes:
                wait_for(act, is_biased, g.lag(2))
            wait_for(act, att_out, g.lag(2))
            for half in range(2):
                ins = act.copy(v[:, g.b, 2 * half:2 * half + 2, :], v_ps[g.b][:, 2 * half:2 * half + 2, 0:D + 2])
            ins.then_inc(v_out.sem, 1)
        run_groups(act, n, [(norm, 0), (out, 1)])

    @block.vector
    def _(dve):
        def out_att(g):
            wait_for(dve, v_out, g)
            wait_for(dve, att_stored, g.lag(2))
            ins = dve.tensor_copy(att[:, g.b], v[:, g.b, :, D:D + 2])
            if not nodes:
                settle(ph, dve, g)
                ins = dve.tensor_copy(K.att[:, cols(g, SUB), 0:2], v[:, g.b, :, D:D + 2])
            ins.then_inc(att_out.sem, 1)

        def count(g):
            wait_for(dve, v_out, g)
            dve.tensor_tensor(biased[:, g.b], v[:, g.b, :, 0:D], to_subs(W.row["gat2_b"]), ALU.add).then_inc(is_biased.sem, 1)
            wait_for(dve, is_biased, g)
            settle(ph, dve, g)
            for s in range(SUB):
                ins = dve.bn_stats(tables["node_stats"][:, cols(g, SUB, s, 1), :], biased[:, g.b, s, :])
            ins.then_inc(counted.sem, 1)
        if nodes:
            run_groups(dve, n, [(out_att, 1), (count, 1)])
        else:
            run_groups(dve, n, [(out_att, 1)])
    ph.close()


def mean_block(nc, K, W, tables):
    ph = Phase(nc, "mean", EG)
    S, A_ = ph.count_sem, ph.dma_sems
    rows4 = [P, 2, SUB, D]
    sums = SegmentSums(ph, K, tables["yv"], K.idx_y, D, [K.inv_deg])
    x_in, y, z = (ph.sb(n, rows4) for n in ("x_in", "y", "z"))
    g_ps = [ph.ps(f"g_ps{b}", [P, GROUP]) for b in range(2)]
    norm = Norm(ph, "norm")
    mean_t = ph.sb("mean_t", [P, 2, 1, GROUP])
    normed, turned, inner, added = (S(n) for n in ("normed", "turned", "inner", "added"))
    loaded, stored = A_("loaded"), A_("stored")
    block = ph.block()

    @block.sync
    def _(sp):
        def load(g):
            wait_for(sp, added, g.lag(2))
            sp.dma_start(x_in[:, g.b], at(slot_rows(tables["x1"]), g)).then_inc(loaded.of(g), 16)

        def store(g):
            wait_for(sp, norm.done, g)
            sp.dma_start(at(slot_rows(tables["x2"]), g), z[:, g.b]).then_inc(stored.of(g), 16)
        run_groups(sp, EG, [(load, 0), (store, 3)])
        wait_for_all(sp, stored)

    @block.gpsimd
    def _(pool):
        run_groups(pool, EG, [(lambda g: sums.pool_fetch(pool, g), 0)])

    @block.tensor
    def _(pe):
        def turn(g):
            wait_for(pe, normed, g)
            wait_for(pe, inner, g.lag(2))
            turn_back(pe, lanes(g_ps[g.b], D), mean_t[:, g.b], range(SUB), K.ident).then_inc(turned.sem, 1)
        run_groups(pe, EG, [(lambda g: sums.tensor_sum(pe, g), 0), (turn, 1)])

    @block.scalar
    def _(act):
        def graph_norm(g):
            wait_for(act, sums.carried, g)
            wait_for(act, turned, g.lag(2))
            act.activation(mean_t[:, g.b, 0, :], sums.sum_t[:, g.b, 0, :], ACT.Identity,
                           bias=W.ln2_shift[:], scale=W.ln2_scale[:]).then_inc(normed.sem, 1)
        run_groups(act, EG, [(graph_norm, 0), (lambda g: sums.scalar_weigh(act, g), -2), (lambda g: norm.scalar_root(act, g, W.eps), 1)])

    @block.vector
    def _(dve):
        sums.vector_zero(dve)

        def add(g):
            wait_for(dve, turned, g)
            wait_for(dve, loaded, g)
            wait_for(dve, norm.done, g.lag(2))
            dve.tensor_tensor(y[:, g.b], lanes(g_ps[g.b], D), x_in[:, g.b], ALU.add).then_inc(inner.sem, 1)
            wait_for(dve, inner, g)
            dve.scalar_tensor_tensor(y[:, g.b], y[:, g.b], 0.0, x_in[:, g.b], ALU.max, ALU.add).then_inc(added.sem, 1)
            wait_for(dve, added, g)
            norm.vector_moments(dve, g, y)

        def apply(g):
            wait_for(dve, stored, g.lag(2))
            norm.vector_apply(dve, g, y, z)
        run_groups(dve, EG, [(lambda g: sums.vector_carry(dve, g, [normed]), 0), (apply, 2), (add, 1)])
    ph.close()



def spread_column(dve, pe_ready, diag, ident, column):
    dve.tensor_scalar(diag[:], ident[:], column, None, ALU.mult).then_inc(pe_ready, 1)


def jk_start_block(nc, K, W, tables):
    ph = Phase(nc, "jk_start", 0)
    row, row_ps = ph.sb("row", [LAYERS, D]), ph.ps("row_ps", [LAYERS, D])
    made, turned, copied, stored = (ph.sem(n) for n in ("made", "turned", "copied", "stored"))
    block = ph.block()

    @block.vector
    def _(dve):
        dve.tensor_scalar(W.jk_const[:], W.jk_b[:], 0.0, None, ALU.max).then_inc(made, 1)
        dve.wait_ge(turned, 1)
        dve.tensor_copy(row[:], row_ps[:]).then_inc(copied, 1)

    @block.tensor
    def _(pe):
        pe.wait_ge(made, 1)
        pe.transpose(row_ps[:], W.jk_const[:], K.ident[:]).then_inc(turned, 1)

    @block.sync
    def _(sp):
        sp.wait_ge(copied, 1)
        for i in range(LAYERS - 1):
            sp.dma_start(tables[f"jk{i}"][SLOTS:SLOTS + 1], row[i:i + 1, :]).then_inc(stored, 16)
        sp.wait_ge(stored, 16 * (LAYERS - 1))
    ph.close()


def jk_layer_block(nc, i, K, W, tables):
    ph = Phase(nc, f"jk_layer{i}", EG)
    S, A_ = ph.count_sem, ph.dma_sems
    last = i == LAYERS - 1
    sums = SegmentSums(ph, K, tables["x2"] if i == 0 else tables[f"jk{i - 1}"], K.idx if i == 0 else K.idx_jk, D, [K.l2_weight])
    h_t, h = ph.sb("h_t", [P, 2, 1, GROUP]), ph.sb("h", [P, 2, SUB, D])
    off, square = ph.sb("off", [P, GROUP]), ph.sb("square", [P, GROUP])
    off_sum, square_sum = ph.sb("off_sum", [P, EG]), ph.sb("square_sum", [P, EG])
    small, diag = ph.sb("small", [P, 4]), [ph.sb(f"diag{b}", [P, P]) for b in range(2)]
    h_ps, rows_ps = ([ph.ps(f"{k}{b}", [P, 1, GROUP]) for b in range(2)] for k in ("h_ps", "rows_ps"))
    made, kept, turned, out_done, offset, counted = (S(n) for n in ("made", "kept", "turned", "out_done", "offset", "counted"))
    scaled, shifted, relued = (S(n) for n in ("scaled", "shifted", "relued"))
    if i:
        ready = ph.sb("ready", [P, 2, SUB, D])
        sums.rows, sums.messages, sums.used = ready, relued, scaled
    ht_stored, h_stored = A_("ht_stored"), A_("h_stored")
    chain, to_root, rooted, diag_ready, spread = (ph.sem(n) for n in ("chain", "to_root", "rooted", "diag_ready", "spread"))
    block = ph.block()

    @block.sync
    def _(sp):
        def store_t(g):
            wait_for(sp, kept, g)
            sp.dma_start(at(tables["jk_t"][:, :, i:i + 1, :], g), h_t[:, g.b]).then_inc(ht_stored.of(g), 16)

        def store(g):
            wait_for(sp, out_done, g)
            settle(ph, sp, g)
            sp.dma_start(at(slot_rows(tables[f"jk{i}"]), g), h[:, g.b]).then_inc(h_stored.of(g), 16)
        run_groups(sp, EG, [(store_t, 2)] + ([] if last else [(store, 3)]))
        wait_for_all(sp, ht_stored)
        if not last:
            wait_for_all(sp, h_stored)

    @block.gpsimd
    def _(pool):
        run_groups(pool, EG, [(lambda g: sums.pool_fetch(pool, g), 0)])

    @block.tensor
    def _(pe):
        def make(g):
            wait_for(pe, sums.carried, g)
            wait_for(pe, kept, g.lag(2))
            layer_t(pe, h_ps[g.b], [(W.jk_w[:, i:i + 1, :], sums.sum_t[:, g.b])]).then_inc(made.sem, 1)

        def turn(g):
            wait_for(pe, kept, g)
            wait_for(pe, out_done, g.lag(2))
            turn_back(pe, lanes(rows_ps[g.b][:, 0, :], D), h_t[:, g.b], range(SUB), K.ident).then_inc(turned.sem, 1)
        run_groups(pe, EG, [(lambda g: sums.tensor_sum(pe, g), 0), (make, 1)] + ([] if last else [(turn, 2)]))
        if not last:
            wait_for(pe, out_done, Group(0, EG - 1))
            for b in range(2):
                pe.wait_ge(diag_ready, b + 1)
                pe.matmul(rows_ps[b][:, 0, 0:D], K.ones[:], diag[b][:], start=True, stop=True).then_inc(spread, 1)

    @block.scalar
    def _(act):
        def relu_messages(g):
            wait_for(act, shifted, g)
            m = ready[:, g.b]
            act.activation(m, m, ACT.Relu).then_inc(relued.sem, 1)

        def keep(g):
            wait_for(act, made, g)
            wait_for(act, ht_stored, g.lag(2))
            wait_for(act, counted, g.lag(2))
            if not last:
                wait_for(act, turned, g.lag(2))
            act.activation(h_t[:, g.b, 0, :], h_ps[g.b][:, 0, :], ACT.Relu, bias=W.jk_b[:, i:i + 1]).then_inc(kept.sem, 1)

        def out(g):
            wait_for(act, turned, g)
            wait_for(act, h_stored, g.lag(2))
            act.copy(h[:, g.b], lanes(rows_ps[g.b][:, 0, :], D)).then_inc(out_done.sem, 1)
        stages = [(keep, 1)] + ([(relu_messages, -1)] if i else []) + [(lambda g: sums.scalar_weigh(act, g), -2)]
        if not last:
            stages.append((out, 2))
        run_groups(act, EG, stages)
        act.wait_ge(to_root, 1)
        act.activation(small[:, 3:4], small[:, 1:2], ACT.Sqrt, bias=W.eps[:]).then_inc(rooted, 1)

    @block.vector
    def _(dve):
        link = linker(dve, chain)
        sums.vector_zero(dve)

        def adjust(g):
            wait_for(dve, sums.arrived, g)
            wait_for(dve, sums.summed, g.lag(2))
            m = ready[:, g.b]
            dve.tensor_tensor(m, sums.msg[:, g.b], to_subs(W.jk_scale_row), ALU.mult).then_inc(scaled.sem, 1)
            wait_for(dve, scaled, g)
            dve.tensor_tensor(m, m, to_subs(W.jk_shift_row), ALU.add).then_inc(shifted.sem, 1)

        def count(g):
            wait_for(dve, kept, g)
            wait_for(dve, counted, g.lag(1))
            dve.scalar_tensor_tensor(off[:], h_t[:, g.b, 0, :], W.jk_const[:, i:i + 1], K.last_row[:, cols(g, GROUP)],
                                     ALU.subtract, ALU.mult, accum_out=off_sum[:, cols(g, 1)]).then_inc(offset.sem, 1)
            wait_for(dve, offset, g)
            dve.scalar_tensor_tensor(square[:], off[:], 1.0, off[:], ALU.mult, ALU.mult,
                                     accum_out=square_sum[:, cols(g, 1)]).then_inc(counted.sem, 1)
        stages = [(lambda g: sums.vector_carry(dve, g, [made]), 0), (count, 1)]
        if i:
            stages.insert(0, (adjust, -1))
        run_groups(dve, EG, stages)
        wait_for(dve, counted, Group(0, EG - 1))
        link(dve.tensor_reduce(small[:, 0:1], off_sum[:], AX.X, ALU.add))
        link(dve.tensor_reduce(small[:, 1:2], square_sum[:], AX.X, ALU.add))
        link(dve.tensor_scalar(small[:, 0:2], small[:, 0:2], 1.0 / N_NODES, None, ALU.mult))
        link(dve.tensor_tensor(small[:, 2:3], small[:, 0:1], small[:, 0:1], ALU.mult))
        link(dve.tensor_tensor(small[:, 1:2], small[:, 1:2], small[:, 2:3], ALU.subtract))
        link(dve.tensor_tensor(small[:, 0:1], small[:, 0:1], W.jk_const[:, i:i + 1], ALU.add))
        dve.sem_inc(to_root, 1)
        dve.wait_ge(rooted, 1)
        link(dve.reciprocal(small[:, 3:4], small[:, 3:4]))
        scale, shift = W.jk_scale[:, i:i + 1], W.jk_shift[:, i:i + 1]
        link(dve.tensor_tensor(scale, small[:, 3:4], W.jk_gamma[:, i:i + 1], ALU.mult))
        link(dve.tensor_tensor(small[:, 0:1], small[:, 0:1], scale, ALU.mult))
        link(dve.tensor_tensor(shift, W.jk_beta[:, i:i + 1], small[:, 0:1], ALU.subtract))
        if not last:
            for b, (column, row) in enumerate(((scale, W.jk_scale_row), (shift, W.jk_shift_row))):
                spread_column(dve, diag_ready, diag[b], K.ident, column)
                dve.wait_ge(spread, b + 1)
                link(dve.tensor_copy(row[:], rows_ps[b][:, 0, 0:D]))
    ph.close()


def lonely_block(nc, K, W):
    ph = Phase(nc, "lonely", 0)
    each, best, result, diag = ph.sb("each", [P, LAYERS]), ph.sb("best", [P, 1]), ph.sb("result", [P, 1]), ph.sb("diag", [P, P])
    lin_ps, row_ps = ph.ps("lin_ps", [P, 1]), ph.ps("row_ps", [P, D])
    chain, best_ready, multiplied, biased, diag_ready, spread = (ph.sem(n) for n in ("chain", "best_ready", "multiplied", "biased", "diag_ready", "spread"))
    block = ph.block()

    @block.vector
    def _(dve):
        link = linker(dve, chain)
        link(dve.tensor_tensor(each[:], W.jk_const[:], W.jk_scale[:], ALU.mult))
        link(dve.tensor_tensor(each[:], each[:], W.jk_shift[:], ALU.add))
        link(dve.tensor_scalar(each[:], each[:], 0.0, None, ALU.max))
        dve.tensor_reduce(best[:], each[:], AX.X, ALU.max).then_inc(best_ready, 1)
        dve.wait_ge(biased, 1)
        spread_column(dve, diag_ready, diag, K.ident, result[:])
        dve.wait_ge(spread, 1)
        link(dve.tensor_copy(W.lonely_row[:], row_ps[:]))

    @block.tensor
    def _(pe):
        pe.wait_ge(best_ready, 1)
        pe.matmul(lin_ps[:], W.m["lin"][:, 0, :], best[:], start=True, stop=True).then_inc(multiplied, 1)
        pe.wait_ge(diag_ready, 1)
        pe.matmul(row_ps[:], K.ones[:], diag[:], start=True, stop=True).then_inc(spread, 1)

    @block.scalar
    def _(act):
        act.wait_ge(multiplied, 1)
        act.activation(result[:], lin_ps[:], ACT.Relu, bias=W.col["lin_b_c"][:]).then_inc(biased, 1)
    ph.close()


def jk_end_block(nc, K, W, tables):
    ph = Phase(nc, "jk_end", EG)
    S, A_ = ph.count_sem, ph.dma_sems
    rows4 = [P, 2, SUB, D]
    layers = ph.sb("layers", [P, 2, LAYERS, GROUP])
    top_t, r_t = ph.sb("top_t", [P, 2, 1, GROUP]), ph.sb("r_t", [P, 2, 1, GROUP])
    x_in, y, z, scaled = (ph.sb(n, rows4) for n in ("x_in", "y", "z", "scaled"))
    r_ps, rows_ps = ([ph.ps(f"{k}{b}", [P, 1, GROUP]) for b in range(2)] for k in ("r_ps", "rows_ps"))
    norm = Norm(ph, "norm")
    loaded, x_loaded, z_stored, s_stored = A_("loaded"), A_("x_loaded"), A_("z_stored"), A_("s_stored")
    normed, maxed, made, kept, turned, added, is_scaled = (S(n) for n in ("normed", "maxed", "made", "kept", "turned", "added", "is_scaled"))
    pair = S("pair", 2)
    block = ph.block()

    @block.sync
    def _(sp):
        def load(g):
            wait_for(sp, maxed, g.lag(2))
            sp.dma_start(layers[:, g.b], at(tables["jk_t"], g)).then_inc(loaded.of(g), 16)

        def load_x(g):
            wait_for(sp, added, g.lag(2))
            settle(ph, sp, g)
            sp.dma_start(x_in[:, g.b], at(slot_rows(tables["x2"]), g)).then_inc(x_loaded.of(g), 16)

        def store(g):
            wait_for(sp, norm.done, g)
            sp.dma_start(at(slot_rows(tables["x3_own"]), g), z[:, g.b]).then_inc(z_stored.of(g), 16)
            wait_for(sp, is_scaled, g)
            sp.dma_start(at(slot_rows(tables["x3"]), g), scaled[:, g.b]).then_inc(s_stored.of(g), 16)
        run_groups(sp, EG, [(store, 4), (load, -2), (load_x, 1)])
        wait_for_all(sp, z_stored)
        wait_for_all(sp, s_stored)

    @block.tensor
    def _(pe):
        def make(g):
            wait_for(pe, maxed, g)
            wait_for(pe, kept, g.lag(2))
            layer_t(pe, r_ps[g.b], [(W.m["lin"], top_t[:, g.b])]).then_inc(made.sem, 1)

        def turn(g):
            wait_for(pe, kept, g)
            wait_for(pe, added, g.lag(2))
            turn_back(pe, lanes(rows_ps[g.b][:, 0, :], D), r_t[:, g.b], range(SUB), K.ident).then_inc(turned.sem, 1)
        run_groups(pe, EG, [(make, 1), (turn, 2)])

    @block.scalar
    def _(act):
        def norms(g):
            wait_for(act, loaded, g)
            for i in range(LAYERS):
                ins = act.activation(layers[:, g.b, i, :], layers[:, g.b, i, :], ACT.Relu,
                                     bias=W.jk_shift[:, i:i + 1], scale=W.jk_scale[:, i:i + 1])
            ins.then_inc(normed.sem, 1)

        def scale(g):
            wait_for(act, norm.done, g)
            wait_for(act, s_stored, g.lag(2))
            settle(ph, act, g)
            for s in range(SUB):
                ins = act.activation(scaled[:, g.b, s, :], z[:, g.b, s, :], ACT.Copy, scale=K.dinv[:, cols(g, SUB, s, 1)])
            ins.then_inc(is_scaled.sem, 1)

        def keep(g):
            wait_for(act, made, g)
            wait_for(act, turned, g.lag(2))
            act.activation(r_t[:, g.b, 0, :], r_ps[g.b][:, 0, :], ACT.Relu, bias=W.col["lin_b_c"][:]).then_inc(kept.sem, 1)
        run_groups(act, EG, [(norms, -1), (keep, 1), (lambda g: norm.scalar_root(act, g, W.eps), 2), (scale, 3)])

    @block.vector
    def _(dve):
        def top(g):
            wait_for(dve, normed, g)
            wait_for(dve, made, g.lag(2))
            dve.tensor_tensor(layers[:, g.b, 0, :], layers[:, g.b, 0, :], layers[:, g.b, 1, :], ALU.max).then_inc(pair.sem, 1)
            dve.tensor_tensor(layers[:, g.b, 2, :], layers[:, g.b, 2, :], layers[:, g.b, 3, :], ALU.max).then_inc(pair.sem, 1)
            wait_for(dve, pair, g)
            dve.tensor_tensor(top_t[:, g.b, 0, :], layers[:, g.b, 0, :], layers[:, g.b, 2, :], ALU.max).then_inc(maxed.sem, 1)

        def add(g):
            wait_for(dve, turned, g)
            wait_for(dve, x_loaded, g)
            wait_for(dve, norm.done, g.lag(2))
            dve.tensor_tensor(y[:, g.b], lanes(rows_ps[g.b][:, 0, :], D), x_in[:, g.b], ALU.add).then_inc(added.sem, 1)
            wait_for(dve, added, g)
            norm.vector_moments(dve, g, y)

        def apply(g):
            wait_for(dve, z_stored, g.lag(2))
            wait_for(dve, is_scaled, g.lag(2))
            norm.vector_apply(dve, g, y, z)
        run_groups(dve, EG, [(apply, 3), (top, 0), (add, 2)])
    ph.close()



def resnorm_gnn(nc, A, out, debug=None):
    def dram(name, rows, width, dt=F32):
        kind = "ExternalOutput" if debug and name in debug else "Internal"
        return nc.dram_tensor(name, [rows, width] if width else [rows], dt, kind=kind).ap()
    both = SLOTS + NODES_PAD
    tables = {"dst": dram("dst_pad", SLOTS + 16, 0, I32), "meta": dram("meta", NODES_PAD, 2)}
    for name, width in (("h1", HID), ("h2", HID), ("u", D), ("att1", 2), ("x2", D), ("x3", D), ("r1", HID), ("r2", HID)):
        tables[name] = dram(name, both, width)
    tables["att2"] = dram("att2", both, 2)
    tables["yv"] = dram("yv", SLOTS + both, D)
    tables["g_t"] = nc.dram_tensor("g_t", [EG, P, 1, GROUP], F32, kind="Internal").ap()
    tables["jk_t"] = nc.dram_tensor("jk_t", [EG, P, LAYERS, GROUP], F32, kind="Internal").ap()
    for i in range(LAYERS):
        tables[f"jk{i}"] = dram(f"jk{i}", SLOTS + 1, D)
    for name in ("x_own", "x_msg", "x1", "x3_own"):
        tables[name] = dram(name, SLOTS, D)
    for name in ("h1_t", "h2_t"):
        tables[name] = nc.dram_tensor(name, [EG, P, 2, GROUP], F32, kind="Internal").ap()
    with ExitStack() as ctx:
        K, W = Constants(nc, ctx), Weights(nc, ctx)
        tables["node_stats"] = ctx.enter_context(nc.sbuf_tensor("node_stats", [P, NG * SUB, 6], F32))
        setup_block(nc, A, K, W, tables)
        node_net_block(nc, "sage", K, W, tables, A["x"], out)
        K.make_room(nc, ctx)
        tables["slot_stats"] = ctx.enter_context(nc.sbuf_tensor("slot_stats", [P, ET, 6], F32))
        maps_block(nc, K, tables)
        with nc.sbuf_tensor("src_meta", [P, ET, 2], F32) as src_meta:
            slot_hidden_block(nc, "sage0", K, W, tables, src_meta)
            meta_block(nc, K, src_meta)
        slot_hidden_block(nc, "sage1", K, W, tables)
        slot_out_block(nc, "sage", K, W, tables, out)
        for number, table in (("1", "att1"), ("2", "att2")):
            if number == "2":
                second_product_block(nc, "node_v", K, W, tables)
                second_product_block(nc, "slot_v", K, W, tables)
            with nc.sbuf_tensor(f"scores{number}", [P, ET, 2], F32) as scores:
                scores_block(nc, f"scores{number}_in", K, tables[table], scores)
                softmax_block(nc, f"softmax{number}", K, scores, 2 if number == "1" else 1)
            attend_block(nc, f"gat{number}", K, W, tables)
            graph_norm_block(nc, f"ln{number}", K, W, tables)
        mean_block(nc, K, W, tables)
        jk_start_block(nc, K, W, tables)
        for i in range(LAYERS):
            jk_layer_block(nc, i, K, W, tables)
        lonely_block(nc, K, W)
        jk_end_block(nc, K, W, tables)
        node_net_block(nc, "gcn", K, W, tables, A["x"], out)
        slot_hidden_block(nc, "gcn0", K, W, tables)
        slot_hidden_block(nc, "gcn1", K, W, tables)
        slot_out_block(nc, "gcn", K, W, tables, out)


_INS = ["x", "src", "dst",
        "L0_gnn_Ws0", "L0_gnn_Wn0", "L0_gnn_b0", "L0_gnn_Ws1", "L0_gnn_Wn1", "L0_gnn_b1", "L0_gnn_Ws2", "L0_gnn_Wn2", "L0_gnn_b2",
        "L1_gnn_W1", "L1_gnn_att_src1", "L1_gnn_att_dst1", "L1_gnn_b1", "L1_gnn_ln1_w", "L1_gnn_ln1_b",
        "L1_gnn_W2", "L1_gnn_att_src2", "L1_gnn_att_dst2", "L1_gnn_b2", "L1_gnn_ln2_w", "L1_gnn_ln2_b",
        "L2_gnn_Ws", "L2_gnn_bs", "L2_gnn_gammas", "L2_gnn_betas", "L2_gnn_lin1_w", "L2_gnn_lin1_b",
        "L3_gnn_W0", "L3_gnn_b0", "L3_gnn_W1", "L3_gnn_b1", "L3_gnn_W2", "L3_gnn_b2"]


def kernel(**inputs):
    import numpy as _np
    import concourse.bacc as _bacc
    from concourse import mybir as _mybir
    from concourse.bass_utils import run_bass_kernel_spmd as _run

    nc = _bacc.Bacc("TRN2", target_bir_lowering=False, num_devices=1)
    arrays, aps = {}, {}
    for name in _INS:
        a = _np.ascontiguousarray(inputs[name])
        arrays[f"in_{name}"] = a
        aps[name] = nc.dram_tensor(f"in_{name}", a.shape, _mybir.dt.from_np(a.dtype), kind="ExternalInput").ap()
    out = nc.dram_tensor("out_0", [N_NODES, D], _mybir.dt.float32, kind="ExternalOutput").ap()
    resnorm_gnn(nc, aps, out)
    r = _run(nc, [arrays], core_ids=[0])
    return r.results[0]["out_0"]
```
